# Optimizing a Trainium2 kernel written in Bass

```python
import numpy as np
import jax
import jax.numpy as jnp

def _softmax(x, axis=-1):
    return jax.nn.softmax(x, axis=axis)

def _gelu(x):
    return jax.nn.gelu(x, approximate=True)

def _silu(x):
    return jax.nn.silu(x)

def _sigmoid(x):
    return jax.nn.sigmoid(x)

def _layernorm(x, axis=-1, eps=1e-05):
    m = jnp.mean(x, axis=axis, keepdims=True)
    v = jnp.var(x, axis=axis, keepdims=True)
    return (x - m) / jnp.sqrt(v + eps)

def _scatter_add(tgt, idx, src, axis=0):
    return tgt.at[idx].add(src)

def _segment_sum(src, seg, n):
    return jax.ops.segment_sum(src, seg, n)
kernel_name = 'mk_adj_ffn_d1_adj_r2_1f863c'

def setup_inputs(seed: int=0):
    np.random.seed(seed)
    _w = jnp.asarray

    def _rec_inputs():
        import jax
        import jax.numpy as jnp
        _gk = jax.random.key(seed)
        x = -0.0002928 + 1 * jax.random.normal(jax.random.fold_in(_gk, 1), (32, 256, 256), jnp.float32)
        _a = jax.random.bernoulli(jax.random.fold_in(_gk, 2), 0.0625, (256, 256))
        adj = _a.astype(jnp.int32)
        return (x, adj)
    x, adj = _rec_inputs()

    def _L0_gnn_setup():
        import jax, jax.numpy as jnp
        import numpy as np
        D_MODEL = 256
        NUM_HEADS = 8
        D_HEAD = D_MODEL // NUM_HEADS
        B, N = (4, 1024)
        key = jax.random.key(seed)
        ks = jax.random.split(key, 10)
        s = 1.0 / np.sqrt(D_MODEL)
        inp = {'h': jax.random.normal(ks[0], (B, N, D_MODEL), dtype=jnp.float32), 'adj': jax.random.randint(ks[1], (N, N), 0, 2, dtype=jnp.int32), 'Wq': jax.random.uniform(ks[2], (D_MODEL, D_MODEL), jnp.float32, -s, s), 'bq': jax.random.uniform(ks[3], (D_MODEL,), jnp.float32, -s, s), 'Wk': jax.random.uniform(ks[4], (D_MODEL, D_MODEL), jnp.float32, -s, s), 'bk': jax.random.uniform(ks[5], (D_MODEL,), jnp.float32, -s, s), 'Wv': jax.random.uniform(ks[6], (D_MODEL, D_MODEL), jnp.float32, -s, s), 'bv': jax.random.uniform(ks[7], (D_MODEL,), jnp.float32, -s, s), 'Wo': jax.random.uniform(ks[8], (D_MODEL, D_MODEL), jnp.float32, -s, s), 'bo': jax.random.uniform(ks[9], (D_MODEL,), jnp.float32, -s, s)}
        return inp
    _L0_gnn_all = _L0_gnn_setup()
    _L0_gnn_in = {k: v for k, v in _L0_gnn_all.items() if k in ('Wq', 'bq', 'Wk', 'bk', 'Wv', 'bv', 'Wo', 'bo')}
    del _L0_gnn_all

    def _L0_ffn_setup():
        import jax, jax.numpy as jnp
        import numpy as np
        NEXPERTS = 16
        key = jax.random.key(seed)
        k1, k2, k3, k4 = jax.random.split(key, 4)
        B, S, D = (4, 1024, 256)
        E, Sets, F = (16, 4, 32)
        scale = 0.02
        return {'x': jax.random.normal(k1, (B, S, D), dtype=jnp.float32), 'controller': jax.random.normal(k2, (D, E, Sets), dtype=jnp.float32) * scale, 'f1': jax.random.normal(k3, (D, E, Sets, F), dtype=jnp.float32) * scale, 'f2': jax.random.normal(k4, (E, Sets, F, D), dtype=jnp.float32) * scale}
    _L0_ffn_all = _L0_ffn_setup()
    _L0_ffn_in = {k: v for k, v in _L0_ffn_all.items() if k in ('controller', 'f1', 'f2')}
    del _L0_ffn_all
    return {'x': x, 'adj': adj, 'L0_gnn_Wq': _L0_gnn_in['Wq'], 'L0_gnn_bq': _L0_gnn_in['bq'], 'L0_gnn_Wk': _L0_gnn_in['Wk'], 'L0_gnn_bk': _L0_gnn_in['bk'], 'L0_gnn_Wv': _L0_gnn_in['Wv'], 'L0_gnn_bv': _L0_gnn_in['bv'], 'L0_gnn_Wo': _L0_gnn_in['Wo'], 'L0_gnn_bo': _L0_gnn_in['bo'], 'L0_ffn_controller': _L0_ffn_in['controller'], 'L0_ffn_f1': _L0_ffn_in['f1'], 'L0_ffn_f2': _L0_ffn_in['f2']}

def reference(x, adj, L0_gnn_Wq, L0_gnn_bq, L0_gnn_Wk, L0_gnn_bk, L0_gnn_Wv, L0_gnn_bv, L0_gnn_Wo, L0_gnn_bo, L0_ffn_controller, L0_ffn_f1, L0_ffn_f2):
    import jax
    import jax.numpy as jnp

    def _L0_gnn_ref(h, adj, Wq, bq, Wk, bk, Wv, bv, Wo, bo):
        import jax, jax.numpy as jnp
        import numpy as np
        D_MODEL = 256
        NUM_HEADS = 8
        D_HEAD = D_MODEL // NUM_HEADS
        B, N = (4, 1024)
        b, n, _ = h.shape

        def split_heads(x):
            return x.reshape(b, n, NUM_HEADS, D_HEAD).transpose(0, 2, 1, 3)
        q = split_heads(h @ Wq.T + bq)
        k = split_heads(h @ Wk.T + bk)
        v = split_heads(h @ Wv.T + bv)
        scale = 1.0 / np.sqrt(D_HEAD)
        scores = jnp.einsum('bhqd,bhkd->bhqk', q, k) * scale
        mask = (adj == 0)[None, None, :, :]
        scores = jnp.where(mask, -jnp.inf, scores)
        attn = jax.nn.softmax(scores, axis=-1)
        out = jnp.einsum('bhqk,bhkd->bhqd', attn, v)
        out = out.transpose(0, 2, 1, 3).reshape(b, n, D_MODEL)
        return out @ Wo.T + bo

    def _L0_ffn_ref(x, controller, f1, f2):
        import jax, jax.numpy as jnp
        import numpy as np
        NEXPERTS = 16
        B, S, D = x.shape
        t = NEXPERTS
        grouped = x.reshape(B, S // t, t, D)
        cont_logits = jnp.einsum('bgtd,des->bgtes', grouped, controller)
        tie = jnp.linspace(0.0, 1e-06, t, dtype=x.dtype).reshape(t, 1, 1)
        cont_logits = cont_logits + tie
        cont_perm = (cont_logits == jnp.max(cont_logits, axis=-3, keepdims=True)).astype(x.dtype)
        intermediate = jnp.einsum('bgtd,desf->bgtesf', grouped, f1)
        inner = jnp.einsum('bgtesf,bgtes->bgesf', intermediate, cont_perm)
        inner = jax.nn.relu(inner)
        inter2 = jnp.einsum('bgesf,esfd->bgesd', inner, f2)
        result = jnp.einsum('bgesd,bgtes->bgtd', inter2, cont_perm)
        return result.reshape(B, S, D)
    x = x + _L0_gnn_ref(_layernorm(x, axis=-1), adj, L0_gnn_Wq, L0_gnn_bq, L0_gnn_Wk, L0_gnn_bk, L0_gnn_Wv, L0_gnn_bv, L0_gnn_Wo, L0_gnn_bo)
    x = x + _L0_ffn_ref(_layernorm(x, axis=-1), L0_ffn_controller, L0_ffn_f1, L0_ffn_f2)
    return x

_drawn_inputs = setup_inputs


def setup_inputs(seed=0):
    import zlib

    import numpy as np

    out = dict(_drawn_inputs(seed))
    spreads = {}
    factors = {'L0_gnn_bq': 28.886, 'L0_gnn_bk': 64.0, 'L0_gnn_bv': 2.804}
    for name, (base, spread) in spreads.items():
        noise = np.random.default_rng([zlib.crc32(name.encode()), seed]).standard_normal(out[name].shape)
        drawn = base * np.exp(spread * noise) if base else spread * noise
        out[name] = jnp.asarray(drawn.astype(out[name].dtype))
    for name, factor in factors.items():
        out[name] = (out[name] * factor).astype(out[name].dtype)
    return out
```

```python
from contextlib import ExitStack

import numpy as np

import concourse.bass as bass
from concourse import mybir

F32 = mybir.dt.float32
BF16 = mybir.dt.bfloat16
I32 = mybir.dt.int32
ALU = mybir.AluOpType
ACT = mybir.ActivationFunctionType
AX = mybir.AxisListType

P = 128
HEADS = 8
EPS = 1e-5
MASKED = -3.0e38
T = 16


def gnn_moe_kernel(nc, x, adj, Wq, bq, Wk, bk, Wv, bv, Wo, bo, controller, f1, f2, out):
    B, N, D = x.shape
    DH = D // HEADS
    KT = D // P
    QT = N // P
    G = HEADS * DH // P
    HPG = P // DH
    PAIRS = HEADS // 2
    SCALE = float(1.0 / np.sqrt(DH))
    TILES = B * N // P
    ES = controller.shape[1] * controller.shape[2]
    F = f1.shape[3]
    CT = 16
    CHUNKS = TILES // CT
    UT = 4
    UNITS = CT // UT
    GPT = P // T
    CG = CT * GPT
    CP = CG // 2
    QUADS = ES // 4
    assert D == 2 * P and N == 2 * P and DH == 32 and ES == 64 and F == 32 and CG == P and B % 4 == 0

    scratch = nc.dram_tensor("scratch", (CHUNKS * CG, ES * D), F32, kind="Internal").ap()

    def by_group(c, q):
        rows = slice(c * CG, c * CG + CG) if isinstance(c, int) else bass.ds(c * CG, CG)
        return scratch[rows, q * 4 * D:(q + 1) * 4 * D]

    def by_expert(c, r):
        rows = slice(c * CG + 16 * r, c * CG + 16 * r + 16) if isinstance(c, int) else bass.ds(c * CG + 16 * r, 16)
        return scratch[rows, :].rearrange("(c two) (e d) -> (two e) c d", two=2, d=D)

    xt = x.rearrange("b (t p) d -> p (b t) d", p=P)
    ot = out.rearrange("b (t p) d -> p (b t) d", p=P)

    with ExitStack() as ctx:
        def sb(name, shape, dt=F32):
            return ctx.enter_context(nc.sbuf_tensor(name, shape, dt))

        def sem(name):
            return ctx.enter_context(nc.semaphore(name))

        X1 = sb("X1", [P, TILES, D])
        f1s = sb("f1s", [P, KT, ES, F])
        ctl = sb("ctl", [P, KT, 2, ES])
        tie = sb("tie", [P, UT * GPT, T])
        ident = sb("ident", [P, P])
        stats = sb("stats", [P, UT, 6])
        mv = sb("mv", [P, UT, 2])
        var = sb("var", [P, UT, 1])
        lnv = sb("lnv", [P, UT, 1])
        seed = sb("seed", [P, UT, 1])
        newt = sb("newt", [P, 2, UT, 1])
        rstd = sb("rstd", [P, UT, 1])

        region = sb("region", [P, KT * ES * CG])
        at = [0]

        def part(*shape):
            n = int(np.prod(shape))
            v = region[:, at[0]:at[0] + n]
            at[0] += n
            names = "abcd"[:len(shape)]
            if len(shape) > 1:
                v = v.rearrange(f"p ({' '.join(names)}) -> p {' '.join(names)}",
                                **{k: s for k, s in zip(names, shape)})
            return v

        KPad = part(2, G, HPG, N)
        PTs = part(HEADS, QT * N)
        Ps = part(2, QT, 2, N)
        WT = part(4, KT, D)
        QTs = part(2, G, N)
        Vs = part(2, QT, D)
        hT = part(KT, N)
        rexp = part(QT, D)
        rbc = part(G, N)
        assert at[0] <= KT * ES * CG
        XS = region[:, :].rearrange("p (k e g) -> p k e g", k=KT, e=ES)
        XR = region[:, :].rearrange("p (c d) -> p c d", c=CP)

        work = sb("work", [P, 2, UT, D])
        h2 = work
        stage = work
        hn = work[:, 0, 0:QT, :]
        OT = work[:, 0, 2:2 + G, :]
        wtmp = work[:, 1, :, :]
        wtmp2 = work[:, 0, :, :]
        h2T = sb("h2T", [P, KT, UT * P])
        LT = h2T[:, 0, :]
        permT = sb("permT", [P, CT * P])
        permBD = sb("permBD", [P, 2, 2, 4, P])
        inner = sb("inner", [P, QUADS, CG])
        f2BD = sb("f2BD", [P, 4, 4, D])

        maskb = sb("maskb", [P, QT, 2, N], BF16)
        identb = sb("identb", [P, P], BF16)
        bqs = sb("bqs", [P, G])
        bks = sb("bks", [P, G])
        bvb = sb("bvb", [P, 2, D])
        bob = sb("bob", [P, 2, D])
        nmax = sb("nmax", [P, 2, QT, 2])
        sums = sb("sums", [P, HEADS, QT])
        rsum = sb("rsum", [P, HEADS, QT])
        nanv = sb("nanv", [P, 2, QT])
        gmax = sb("gmax", [P, UT * GPT])
        adjs = permT[:, 0:QT * N].bitcast(I32).rearrange("p (t k) -> p t k", t=QT)
        adjf = permT[:, 512:512 + QT * N].rearrange("p (t k) -> p t k", t=QT)

        bank = [ctx.enter_context(nc.psum_tensor(f"bank{i}", [P, 512], F32)) for i in range(8)]
        S = bank[0:4]
        PTb = bank[4:6]
        Ob = bank[6]
        M = bank[7]

        w_in = sem("w_in")
        ffn_in = sem("ffn_in")
        x_in = [sem("x_in0"), sem("x_in1")]
        consts = sem("consts")
        zeroed = sem("zeroed")
        setup_dve = sem("setup_dve")
        wt_ready = sem("wt_ready")
        wt_saved = sem("wt_saved")
        dve_chain = sem("dve_chain")
        act_chain = sem("act_chain")
        var_done = sem("var_done")
        seed_done = sem("seed_done")
        ln_done = sem("ln_done")
        bo_added = sem("bo_added")
        hT_ready, hT_saved = sem("hT_ready"), sem("hT_saved")
        q_ready, q_saved = sem("q_ready"), sem("q_saved")
        k_ready, k_saved = sem("k_ready"), sem("k_saved")
        v_ready, v_saved = sem("v_ready"), sem("v_saved")
        s_ready = sem("s_ready")
        max_done = sem("max_done")
        exp_done = sem("exp_done")
        pt_ready = sem("pt_ready")
        pt_dve = sem("pt_dve")
        pt_act = sem("pt_act")
        pv_ready = sem("pv_ready")
        rexp_done = sem("rexp_done")
        rbc_ready, rbc_saved = sem("rbc_ready"), sem("rbc_saved")
        onorm_done = sem("onorm_done")
        wo_ready = sem("wo_ready")
        res_done = sem("res_done")
        h2_done = sem("h2_done")
        h2T_ready, h2T_saved = sem("h2T_ready"), sem("h2T_saved")
        log_ready, perm_done = sem("log_ready"), sem("perm_done")
        pbt_ready = sem("pbt_ready")
        pbd_dve, pbd_act = sem("pbd_dve"), sem("pbd_act")
        sel_ready = sem("sel_ready")
        sel_dve, sel_act = sem("sel_dve"), sem("sel_act")
        in_ready = sem("in_ready")
        in_dve, in_act = sem("in_dve"), sem("in_act")
        f2bd_in = [sem(f"f2bd_in{i}") for i in range(4)]
        f2_ready = sem("f2_ready")
        st_dve, st_act = sem("st_dve"), sem("st_act")
        moved = [sem("moved0"), sem("moved1")]
        gathered = [sem("gathered0"), sem("gathered1")]
        sc_ready = sem("sc_ready")
        fin_done = sem("fin_done")
        out_done = sem("out_done")

        block = ctx.enter_context(nc.Block())

        def wait(eng, s, value):
            if isinstance(value, int) and value <= 0:
                return
            eng.wait_ge(s, value)

        def batches(eng, body):
            body(0, 0, False)
            body(1, 1, False)
            with eng.Fori(1, B // 2 - 1) as i:
                for par in range(2):
                    body(i * 2 + par, par, False)
            body(B - 2, 0, False)
            body(B - 1, 1, True)

        def prev(b):
            return b - 1

        def copy_selected(copy, u, t, k, ps):
            tile = u * UT + t
            src = ps[:, :].rearrange("p (g e) -> p g e", e=ES)
            return copy(XS[:, k, :, GPT * tile:GPT * tile + GPT].rearrange("p e g -> p g e"), src)

        @block.sync
        def _(sp):
            for k, W in enumerate((Wq, Wk)):
                sp.dma_start(wtmp[:, 2 * k:2 * k + 2, :], W.rearrange("(t p) i -> p t i", p=P)).then_inc(w_in, 16)
            for k, W in enumerate((Wv, Wo)):
                sp.dma_start(wtmp2[:, 2 * k:2 * k + 2, :], W.rearrange("(t p) i -> p t i", p=P)).then_inc(w_in, 16)
            sp.dma_start(adjs, adj.rearrange("(t p) k -> p t k", p=P)).then_inc(w_in, 16)
            sp.dma_start(X1[:, 0:QT, :], xt[:, 0:QT, :]).then_inc(x_in[0], 16)
            sp.dma_start(X1[:, QT:2 * QT, :], xt[:, QT:2 * QT, :]).then_inc(x_in[1], 16)
            with sp.Fori(1, B // 2) as i:
                for par in range(2):
                    sp.wait_ge(x_in[par], i * 16)
                    b = i * 2 + par
                    sp.dma_start(X1[:, bass.ds(b * QT, QT), :], xt[:, bass.ds(b * QT, QT), :]).then_inc(x_in[par], 16)
            sp.dma_start(f1s[:, :, :, :], f1.rearrange("(t p) e s f -> p t (e s) f", p=P)).then_inc(ffn_in, 16)
            for half in range(2):
                sp.dma_start(ctl[:, :, half, :], controller.rearrange("(t p) e s -> p t (e s)", p=P)).then_inc(ffn_in, 16)

            f2v = f2.rearrange("e s f d -> (e s) f d").rearrange("(q j) f d -> q j f d", j=4)

            def load_f2(c, q):
                wait(sp, f2_ready, (c * QUADS + q) * 2 - 6)
                for j in range(4):
                    sp.dma_start(f2BD[32 * j:32 * j + 32, q % 4, j, :], f2v[q, j]).then_inc(f2bd_in[q % 4], 16)

            def move(c, q):
                n = c * QUADS + q
                wait(sp, st_dve, n + 1)
                wait(sp, st_act, n + 1)
                sp.dma_start(by_group(c, q), stage[:, q % 2, :, :]).then_inc(moved[q % 2], 16)

            def gather(c, r):
                if r == 0:
                    for m in moved:
                        wait(sp, m, (c + 1) * (QUADS // 2) * 16)
                sp.dma_start(XR[:, 8 * r:8 * r + 8, :], by_expert(c, r)).then_inc(gathered[r % 2], 16)

            def chunk(c):
                for q in range(3):
                    load_f2(c, q)
                for q in range(QUADS):
                    if q + 3 < QUADS:
                        load_f2(c, q + 3)
                    move(c, q)
                for r in range(CP // 8):
                    if r > 1:
                        wait(sp, gathered[r % 2], (c * (CP // 16) + r // 2) * 16)
                    gather(c, r)
                for s in range(CT // 2):
                    n = c * (CT // 2) + s
                    wait(sp, fin_done, n + 1)
                    tiles = slice(2 * n, 2 * n + 2) if isinstance(n, int) else bass.ds(n * 2, 2)
                    sp.dma_start(ot[:, tiles, :], X1[:, tiles, :]).then_inc(out_done, 16)
            sp.wait_ge(zeroed, 3)
            chunk(0)
            with sp.Fori(1, CHUNKS) as c:
                chunk(c)
            sp.wait_ge(out_done, CHUNKS * (CT // 2) * 16)

        @block.gpsimd
        def _(pool):
            nc.gpsimd.memset(ident[:, :], 0.0).then_inc(consts, 1)
            nc.gpsimd.memset(identb[:, :], 0.0).then_inc(consts, 1)
            pool.wait_ge(consts, 2)
            for m in (ident, identb):
                nc.gpsimd.affine_select(out=m[:, :], in_=m[:, :], compare_op=ALU.not_equal, fill=1.0, base=0,
                                        pattern=[[-1, P]], channel_multiplier=1).then_inc(consts, 1)
            nc.gpsimd.memset(KPad, 0.0).then_inc(zeroed, 1)
            nc.gpsimd.memset(permBD[:, :, :, :, :], 0.0).then_inc(zeroed, 1)
            nc.gpsimd.memset(f2BD[:, :, :, :], 0.0).then_inc(zeroed, 1)
            values = np.linspace(0.0, 1e-6, T).astype(np.float32)
            for t in range(T):
                nc.gpsimd.memset(tie[:, :, t], float(values[t])).then_inc(zeroed, 1)
            pool.wait_ge(setup_dve, 1)
            nc.gpsimd.memset(permT[:, :], 0.0).then_inc(zeroed, 1)

            pool.wait_ge(w_in, 16 * 9)

            def add_bo(b, par, last):
                wait(pool, ln_done, b + 1)
                xb = X1[:, bass.ds(b * QT, QT), :] if not isinstance(b, int) else X1[:, b * QT:b * QT + QT, :]
                nc.gpsimd.tensor_tensor(xb, xb, bob[:, :, :], ALU.add).then_inc(bo_added, 1)
            batches(pool, add_bo)

        @block.tensor
        def _(pe):
            pe.wait_ge(consts, 4)
            pe.wait_ge(w_in, 16 * 9)
            for k in range(4):
                src = wtmp if k < 2 else wtmp2
                for ob in range(KT):
                    for ib in range(KT):
                        last = nc.tensor.transpose(bank[k][:, ib * D + ob * P:ib * D + ob * P + P],
                                                   src[:, 2 * (k % 2) + ob, ib * P:ib * P + P], ident[:, :])
                last.then_inc(wt_ready, 1)
            pe.wait_ge(wt_saved, 4)

            def h_transpose(b):
                wait(pe, ln_done, b + 1)
                wait(pe, res_done, b - 1)
                for t in range(QT):
                    for k in range(KT):
                        last = nc.tensor.transpose(M[:, k * N + t * P:k * N + t * P + P],
                                                   hn[:, t, k * P:k * P + P], ident[:, :])
                last.then_inc(hT_ready, 1)

            def project(w, ready):
                for g in range(G):
                    for k in range(KT):
                        last = nc.tensor.matmul(M[:, g * N:g * N + N], WT[:, w, k, g * P:g * P + P], hT[:, k, :],
                                                start=(k == 0), stop=(k == KT - 1))
                last.then_inc(ready, 1)

            def q_project(b):
                wait(pe, hT_saved, b + 1)
                project(0, q_ready)

            def k_project(b):
                wait(pe, q_saved, b + 1)
                project(1, k_ready)

            def v_project(b):
                wait(pe, k_saved, b + 1)
                for t in range(QT):
                    for k in range(KT):
                        last = nc.tensor.matmul(M[:, t * D:t * D + D], hT[:, k, t * P:t * P + P], WT[:, 2, k, :],
                                                start=(k == 0), stop=(k == KT - 1))
                last.then_inc(v_ready, 1)

            def scores(b, par, pr):
                g, j = divmod(2 * pr, HPG)
                if pr == 0:
                    wait(pe, q_saved, b + 1)
                    wait(pe, k_saved, b + 1)
                for t in range(QT):
                    n = 2 * pr + t
                    wait(pe, exp_done, b * 8 + n - 3)
                    s = S[n % 4]
                    nc.tensor.matmul(s[:, :], identb[:, :], maskb[:, t, :, :], start=True, stop=False)
                    nc.tensor.matmul(s[:, :], QTs[:, par, g, t * P:t * P + P], KPad[:, par, g, j:j + 2, :],
                                     start=False, stop=True).then_inc(s_ready, 1)

            def p_transpose(b, par, pr):
                wait(pe, exp_done, b * 8 + 2 * pr + 2)
                for h in (2 * pr, 2 * pr + 1):
                    o = h - 2
                    bb, o = (b, o) if o >= 0 else (prev(b), o + 8)
                    if o % 4 == 3:
                        wait(pe, pt_act, bb * 2 + o // 4 + 1)
                    else:
                        wait(pe, pt_dve, bb * 6 + (o // 4) * 3 + o % 4 + 1)
                    for k in range(QT):
                        for t in range(QT):
                            last = nc.tensor.transpose(PTb[h % 2][:, k * N + t * P:k * N + t * P + P],
                                                       Ps[:, pr % 2, t, h % 2, k * P:k * P + P], ident[:, :])
                    last.then_inc(pt_ready, 1)

            def pv(b, par, g):
                wait(pe, pt_dve, b * 6 + 3 * g + 3)
                wait(pe, pt_act, b * 2 + g + 1)
                if g == 0:
                    wait(pe, onorm_done, b)
                    wait(pe, v_saved, b + 1)
                for k in range(QT):
                    for j in range(HPG):
                        h = g * HPG + j
                        last = nc.tensor.matmul(Ob[32 * j:32 * j + 32, g * N:g * N + N],
                                                Vs[:, par, k, h * DH:h * DH + DH], PTs[:, h, k * N:k * N + N],
                                                start=(k == 0), stop=(k == QT - 1))
                last.then_inc(pv_ready, 1)

            def r_transpose(b):
                wait(pe, rexp_done, b + 1)
                if isinstance(b, int) and b == B - 1:
                    wait(pe, res_done, b)
                else:
                    wait(pe, v_saved, b + 2)
                for g in range(G):
                    for t in range(QT):
                        last = nc.tensor.transpose(M[:, g * N + t * P:g * N + t * P + P],
                                                   rexp[:, t, g * P:g * P + P], ident[:, :])
                last.then_inc(rbc_ready, 1)

            def o_project(b):
                wait(pe, onorm_done, b + 1)
                wait(pe, rbc_saved, b + 1)
                for t in range(QT):
                    for g in range(G):
                        last = nc.tensor.matmul(M[:, t * D:t * D + D], OT[:, g, t * P:t * P + P], WT[:, 3, g, :],
                                                start=(g == 0), stop=(g == G - 1))
                last.then_inc(wo_ready, 1)

            h_transpose(0)
            q_project(0)
            k_project(0)
            v_project(0)

            def batch(b, par, last):
                first = isinstance(b, int) and b == 0
                scores(b, par, 0)
                if not first:
                    r_transpose(prev(b))
                scores(b, par, 1)
                p_transpose(b, par, 0)
                if not first:
                    o_project(prev(b))
                scores(b, par, 2)
                p_transpose(b, par, 1)
                if not last:
                    h_transpose(b + 1)
                pv(b, par, 0)
                scores(b, par, 3)
                if not last:
                    q_project(b + 1)
                p_transpose(b, par, 2)
                if not last:
                    k_project(b + 1)
                p_transpose(b, par, 3)
                if not last:
                    v_project(b + 1)
                pv(b, par, 1)
            batches(pe, batch)
            r_transpose(B - 1)
            o_project(B - 1)

            pe.wait_ge(ffn_in, 16 * 3)
            pe.wait_ge(zeroed, 4 + T)
            pe.wait_ge(res_done, B)

            def front(c, u):
                n = c * UNITS + u
                wait(pe, h2_done, n + 1)
                if u == 0:
                    wait(pe, fin_done, c * (CT // 2))
                for k in range(KT):
                    for t in range(UT):
                        last = nc.tensor.transpose(bank[k][:, t * P:t * P + P],
                                                   h2[:, u % 2, t, k * P:k * P + P], ident[:, :])
                last.then_inc(h2T_ready, 1)
                wait(pe, h2T_saved, n + 1)
                for k in range(KT):
                    last = nc.tensor.matmul(bank[2][:, :], ctl[:, k, :, :], h2T[:, k, :],
                                            start=(k == 0), stop=(k == KT - 1))
                last.then_inc(log_ready, 1)

            def one_hot_transpose(c, u):
                n = c * UNITS + u
                wait(pe, perm_done, n + 1)
                wait(pe, pbd_dve, 2 * n)
                wait(pe, pbd_act, 2 * n)
                for t in range(UT):
                    tok = (u * UT + t) * P
                    last = nc.tensor.transpose(bank[3][:, t * P:t * P + P], permT[:, tok:tok + P], ident[:, :])
                last.then_inc(pbt_ready, 1)

            def select(c, u, half):
                n = c * UNITS + u
                wait(pe, pbd_dve, 2 * n + half + 1)
                wait(pe, pbd_act, 2 * n + half + 1)
                for t in (2 * half, 2 * half + 1):
                    for k in range(KT):
                        m = 2 * t + k
                        wait(pe, sel_dve if m % 2 == 0 else sel_act, n * 4 + (m - 4) // 2 + 1)
                        if u == 0 and m < 4:
                            wait(pe, st_dve, c * QUADS)
                            wait(pe, st_act, c * QUADS)
                        nc.tensor.matmul(bank[4 + m % 4][:, :], h2[:, u % 2, t, k * P:k * P + P],
                                         permBD[:, half, t % 2, :, :], start=True, stop=True).then_inc(sel_ready, 1)

            def expand(c, i):
                for qq in range(4):
                    q = 4 * i + qq
                    for k in range(KT):
                        for j in range(4):
                            es = 4 * q + j
                            last = nc.tensor.matmul(bank[i][32 * j:32 * j + 32, qq * CG:qq * CG + CG],
                                                    f1s[:, k, es, :], XS[:, k, es, :],
                                                    start=(k == 0), stop=(k == KT - 1))
                last.then_inc(in_ready, 1)

            def contract(c, q):
                n = c * QUADS + q
                if q % 4 == 0:
                    i = q // 4
                    wait(pe, in_dve if i % 2 else in_act, c * 2 + i // 2 + 1)
                wait(pe, f2bd_in[q % 4], (c * 4 + q // 4 + 1) * 64)
                for hf in range(2):
                    m = 2 * (q % 2) + hf
                    wait(pe, st_act if hf else st_dve, n - 1)
                    nc.tensor.matmul(bank[4 + m][:, :], inner[:, q, :], f2BD[:, q % 4, 2 * hf:2 * hf + 2, :],
                                     start=True, stop=True).then_inc(f2_ready, 1)

            def scatter(c):
                pe.wait_ge(in_dve, (c + 1) * 2)
                pe.wait_ge(in_act, (c + 1) * 2)
                for s in range(CT // 2):
                    n = c * (CT // 2) + s
                    if s >= 4:
                        wait(pe, fin_done, n - 3)
                    wait(pe, gathered[s % 2], (c * (CP // 16) + s // 2 + 1) * 16)
                    for tt in range(2):
                        for j in range(4):
                            pr = (2 * s + tt) * 4 + j
                            last = nc.tensor.matmul(bank[s % 4][32 * j:32 * j + 32, tt * D:tt * D + D],
                                                    permT[:, pr * 32:pr * 32 + 32], XR[:, pr, :],
                                                    start=True, stop=True)
                    last.then_inc(sc_ready, 1)

            def chunk(c):
                front(c, 0)
                one_hot_transpose(c, 0)
                for u in range(UNITS):
                    if u + 1 < UNITS:
                        front(c, u + 1)
                    select(c, u, 0)
                    select(c, u, 1)
                    if u + 1 < UNITS:
                        one_hot_transpose(c, u + 1)
                pe.wait_ge(sel_dve, (c + 1) * UNITS * 4)
                pe.wait_ge(sel_act, (c + 1) * UNITS * 4)
                for i in range(4):
                    expand(c, i)
                for q in range(QUADS):
                    contract(c, q)
                scatter(c)
            chunk(0)
            with pe.Fori(1, CHUNKS) as c:
                chunk(c)

        @block.scalar
        def _(act):
            for t, b in ((bqs, bq), (bks, bk)):
                act.dma_start(t[:, :], b.rearrange("(g p) -> p g", p=P), allow_slow_non_contiguous=True).then_inc(w_in, 16)
            act.dma_start(bvb[:, :, :], bv.partition_broadcast(P).unsqueeze(1).broadcast_to([P, 2, D])).then_inc(w_in, 16)
            act.dma_start(bob[:, :, :], bo.partition_broadcast(P).unsqueeze(1).broadcast_to([P, 2, D])).then_inc(w_in, 16)
            act.wait_ge(w_in, 16 * 9)
            nc.scalar.mul(bqs[:, :], bqs[:, :], SCALE).then_inc(act_chain, 1)
            for k in range(4):
                act.wait_ge(wt_ready, k + 1)
                nc.scalar.copy(WT[:, k, :, :], bank[k][:, :]).then_inc(wt_saved, 1)
            act.wait_ge(act_chain, 1)
            act.wait_ge(zeroed, 1)

            def save_hT(b):
                wait(act, hT_ready, b + 1)
                nc.scalar.copy(hT, M[:, :]).then_inc(hT_saved, 1)

            def save_q(b, par):
                wait(act, q_ready, b + 1)
                for g in range(G):
                    last = nc.scalar.activation(QTs[:, par, g, :], M[:, g * N:g * N + N], ACT.Identity,
                                                bias=bqs[:, g:g + 1], scale=SCALE)
                last.then_inc(q_saved, 1)

            def save_k(b, par):
                wait(act, k_ready, b + 1)
                for g in range(G):
                    for j in range(HPG):
                        r = slice(32 * j, 32 * j + 32)
                        last = nc.scalar.activation(KPad[r, par, g, j, :], M[r, g * N:g * N + N], ACT.Identity,
                                                    bias=bks[r, g:g + 1])
                last.then_inc(k_saved, 1)

            def exps(b, pr):
                if pr < 2:
                    wait(act, pt_ready, b * 8 + 4 * (pr // 2) + 2 * pr - 2)
                else:
                    wait(act, pt_ready, b * 8 + 2 * (pr - 2) + 2)
                if pr == 0:
                    wait(act, rexp_done, b)
                for t in range(QT):
                    wait(act, max_done, b * 8 + 2 * pr + t + 1)
                    for h in range(2):
                        last = nc.scalar.activation(Ps[:, pr % 2, t, h, :], S[(2 * pr + t) % 4][:, h * N:h * N + N],
                                                    ACT.Exp, bias=nmax[:, pr % 2, t, h:h + 1],
                                                    accum_out=sums[:, 2 * pr + h, t:t + 1])
                    last.then_inc(exp_done, 1)

            def save_pt(b, h):
                wait(act, pt_ready, b * 8 + h + 1)
                wait(act, pv_ready, 2 * b + h // 4 - 1)
                nc.scalar.copy(PTs[:, h, :], PTb[h % 2][:, :]).then_inc(pt_act, 1)

            def save_rbc(b):
                wait(act, rbc_ready, b + 1)
                nc.scalar.copy(rbc, M[:, :]).then_inc(rbc_saved, 1)

            def seeds(turn, n):
                wait(act, var_done, turn + 1)
                nc.scalar.activation(lnv[:, 0:n, :], var[:, 0:n, :], ACT.Ln).then_inc(act_chain, 1)
                wait(act, act_chain, turn + 2)
                nc.scalar.activation(seed[:, 0:n, :], lnv[:, 0:n, :], ACT.Exp, scale=-0.5).then_inc(seed_done, 1)

            seeds(0, QT)
            save_hT(0)
            save_q(0, 0)
            save_k(0, 0)

            def batch(b, par, last):
                first = isinstance(b, int) and b == 0
                exps(b, 0)
                if not last:
                    seeds(b + 1, QT)
                if not first:
                    save_rbc(prev(b))
                exps(b, 1)
                exps(b, 2)
                save_pt(b, 3)
                if not last:
                    save_hT(b + 1)
                exps(b, 3)
                if not last:
                    save_q(b + 1, 1 - par)
                    save_k(b + 1, 1 - par)
                save_pt(b, 7)
            batches(act, batch)
            save_rbc(B - 1)

            def save_h2T(c, u):
                n = c * UNITS + u
                wait(act, h2T_ready, n + 1)
                wait(act, perm_done, n)
                for k in range(KT):
                    last = nc.scalar.copy(h2T[:, k, :], bank[k][:, :])
                last.then_inc(h2T_saved, 1)

            def save_one_hot(c, u, half):
                n = c * UNITS + u
                wait(act, pbt_ready, n + 1)
                wait(act, sel_ready, n * 8 - 4 + 4 * half)
                for j in (0, 1):
                    r = slice(32 * j, 32 * j + 32)
                    src = bank[3][r, half * 2 * P:(half + 1) * 2 * P].rearrange("p (t e) -> p t e", t=2)
                    last = nc.scalar.copy(permBD[r, half, :, j, :], src)
                last.then_inc(pbd_act, 1)

            def save_selected(c, u, m):
                n = c * UNITS + u
                wait(act, sel_ready, n * 8 + m + 1)
                if u == 0 and m == 1:
                    wait(act, sc_ready, c * (CT // 2))
                t, k = divmod(m, 2)
                copy_selected(nc.scalar.copy, u, t, k, bank[4 + m % 4]).then_inc(sel_act, 1)

            def chunk(c):
                seeds(c * UNITS + B, UT)
                save_h2T(c, 0)
                save_one_hot(c, 0, 0)
                save_one_hot(c, 0, 1)
                seeds(c * UNITS + (B + 1), UT)
                for u in range(UNITS):
                    if u + 1 < UNITS:
                        save_h2T(c, u + 1)
                    for m in (1, 3, 5, 7):
                        save_selected(c, u, m)
                    if u + 1 < UNITS:
                        save_one_hot(c, u + 1, 0)
                        save_one_hot(c, u + 1, 1)
                    if u + 2 < UNITS:
                        seeds(c * UNITS + (B + u + 2), UT)
                for i in (0, 2):
                    wait(act, in_ready, c * 4 + i + 1)
                    nc.scalar.activation(inner[:, 4 * i:4 * i + 4, :], bank[i][:, :], ACT.Relu).then_inc(in_act, 1)
                for q in range(QUADS):
                    wait(act, f2_ready, (c * QUADS + q) * 2 + 2)
                    wait(act, moved[q % 2], (c * (QUADS // 2) + q // 2) * 16)
                    nc.scalar.copy(stage[:, q % 2, 2:4, :], bank[4 + 2 * (q % 2) + 1][:, :]).then_inc(st_act, 1)
            act.wait_ge(zeroed, 4 + T)
            chunk(0)
            with act.Fori(1, CHUNKS) as c:
                chunk(c)

        @block.vector
        def _(dve):
            chain = [0, 0]

            def link(ins):
                chain[1] += 1
                ins.then_inc(dve_chain, 1)
                dve.wait_ge(dve_chain, chain[0] + chain[1])

            dve.wait_ge(w_in, 16 * 9)
            link(nc.vector.tensor_scalar(adjf, adjs, 0, None, ALU.not_equal))
            link(nc.vector.tensor_reduce(nanv[:, 0, :], adjf, AX.X, ALU.max))
            link(nc.vector.reciprocal(nanv[:, 1, :], nanv[:, 0, :]))
            link(nc.vector.tensor_tensor(nanv[:, 1, :], nanv[:, 1, :], nanv[:, 0, :], ALU.mult))
            for h in range(2):
                last = nc.vector.tensor_scalar(maskb[:, :, h, :], adjf, 0.0, MASKED, ALU.is_equal, ALU.mult)
            last.then_inc(setup_dve, 1)
            dve.wait_ge(wt_ready, 4)

            def statistics(n, tile):
                for t in range(n):
                    last = nc.vector.bn_stats(stats[:, t, :], tile(t))
                link(last)
                nc.vector.memset(newt[:, 0, 0, :], 0.0)
                for t in range(n):
                    last = nc.vector.bn_aggr(mv[:, t, :], stats[:, t, :])
                link(last)
                nc.vector.tensor_scalar(var[:, 0:n, :], mv[:, 0:n, 1:2], EPS, None, ALU.add).then_inc(var_done, 1)

            def norm(n, turn, tile, dst):
                wait(dve, seed_done, turn + 1)
                y = seed[:, 0:n, :]
                link(nc.vector.scalar_tensor_tensor(newt[:, 0, 0:n, :], y, -0.5, y, ALU.mult, ALU.mult))
                link(nc.vector.tensor_tensor(newt[:, 1, 0:n, :], newt[:, 0, 0:n, :], var[:, 0:n, :], ALU.mult))
                link(nc.vector.scalar_tensor_tensor(rstd[:, 0:n, :], newt[:, 1, 0:n, :], 1.5, y, ALU.add, ALU.mult))
                for t in range(n):
                    last = nc.vector.tensor_scalar(dst(t), tile(t), mv[:, t, 0:1], rstd[:, t, 0:1],
                                                   ALU.subtract, ALU.mult)
                return last

            def xtile(i):
                return X1[:, i, :] if isinstance(i, int) else X1[:, bass.ds(i, 1), :].rearrange("p o d -> p (o d)")

            def xbatch(b):
                return X1[:, b * QT:b * QT + QT, :] if isinstance(b, int) else X1[:, bass.ds(b * QT, QT), :]

            def batch_statistics(b, par):
                wait(dve, x_in[par], (b // 2) * 16 + 16 if isinstance(b, int) else (b - par) * 8 + 16)
                statistics(QT, lambda t: xtile(b * QT + t))

            def layer_norm(b):
                wait(dve, hT_ready, b)
                norm(QT, b, lambda t: xtile(b * QT + t), lambda t: hn[:, t, :]).then_inc(ln_done, 1)

            def save_v(b, par):
                wait(dve, v_ready, b + 1)
                nc.vector.tensor_tensor(Vs[:, par, :, :], M[:, :].rearrange("p (t d) -> p t d", t=QT), bvb[:, :, :],
                                        ALU.add).then_inc(v_saved, 1)

            def maxima(b, pr):
                for t in range(QT):
                    n = 2 * pr + t
                    wait(dve, s_ready, b * 8 + n + 1)
                    wait(dve, exp_done, b * 8 + n - 3)
                    nc.vector.tensor_reduce(nmax[:, pr % 2, t, :], S[n % 4][:, :].rearrange("p (h k) -> p h k", h=2),
                                            AX.X, ALU.max, negate=True).then_inc(max_done, 1)

            def save_pt(b, h):
                wait(dve, pt_ready, b * 8 + h + 1)
                wait(dve, pv_ready, 2 * b + h // 4 - 1)
                nc.vector.tensor_copy(PTs[:, h, :], PTb[h % 2][:, :]).then_inc(pt_dve, 1)

            def reciprocals(b):
                wait(dve, exp_done, b * 8 + 8)
                link(nc.vector.reciprocal(rsum[:, :, :], sums[:, :, :]))
                for t in range(QT):
                    last = nc.vector.tensor_scalar(
                        rexp[:, t, :].rearrange("p (h d) -> p h d", h=HEADS),
                        rsum[:, :, t:t + 1].broadcast_to([P, HEADS, DH]), nanv[:, 1, t:t + 1], None, ALU.mult)
                last.then_inc(rexp_done, 1)

            def normalise(b):
                wait(dve, rbc_saved, b + 1)
                wait(dve, pv_ready, 2 * b + 2)
                nc.vector.tensor_tensor(OT, Ob[:, :].rearrange("p (g q) -> p g q", g=G), rbc, ALU.mult)\
                    .then_inc(onorm_done, 1)

            def residual(b):
                wait(dve, wo_ready, b + 1)
                wait(dve, bo_added, b + 1)
                xb = xbatch(b)
                nc.vector.tensor_tensor(xb, xb, M[:, :].rearrange("p (t d) -> p t d", t=QT), ALU.add)\
                    .then_inc(res_done, 1)

            batch_statistics(0, 0)
            layer_norm(0)
            save_v(0, 0)
            before = chain[1]
            LINKS = 6

            def batch(b, par, last):
                first = isinstance(b, int) and b == 0
                chain[0], chain[1] = (before if first else b * LINKS + (before - 1)), 0
                if not first:
                    reciprocals(prev(b))
                maxima(b, 0)
                if not last:
                    batch_statistics(b + 1, 1 - par)
                maxima(b, 1)
                if not last:
                    layer_norm(b + 1)
                if not first:
                    normalise(prev(b))
                save_pt(b, 0)
                save_pt(b, 1)
                maxima(b, 2)
                if not first:
                    residual(prev(b))
                save_pt(b, 2)
                maxima(b, 3)
                save_pt(b, 4)
                save_pt(b, 5)
                save_pt(b, 6)
                if not last:
                    save_v(b + 1, 1 - par)
            batches(dve, batch)
            chain[0], chain[1] = (B - 1) * LINKS + before, 0
            reciprocals(B - 1)
            normalise(B - 1)
            residual(B - 1)
            base = chain[0] + chain[1]
            dve.wait_ge(res_done, B)

            def norm_unit(c, u):
                n = c * UNITS + u
                first = c * CT + u * UT
                statistics(UT, lambda t: xtile(first + t))
                wait(dve, sel_ready, n * 8 - 8)
                if u < 2:
                    wait(dve, moved[u % 2], c * (QUADS // 2) * 16)
                norm(UT, n + B, lambda t: xtile(first + t), lambda t: h2[:, u % 2, t, :]).then_inc(h2_done, 1)

            def one_hot(c, u):
                n = c * UNITS + u
                wait(dve, log_ready, n + 1)
                if u == 0:
                    wait(dve, sc_ready, c * (CT // 2))
                link(nc.vector.tensor_tensor(LT.rearrange("p (g t) -> p g t", t=T),
                                             bank[2][:, :].rearrange("p (g t) -> p g t", t=T), tie[:, :, :], ALU.add))
                link(nc.vector.tensor_reduce(gmax[:, :], LT.rearrange("p (g t) -> p g t", t=T), AX.X, ALU.max))
                for half in range(2):
                    r = slice(64 * half, 64 * half + 64)

                    def odd(v):
                        return v.rearrange("p (c two t) -> p c two t", two=2, t=T)[:, :, half, :]
                    top = gmax[r, :].rearrange("p (c two) -> p c two", two=2)[:, :, half:half + 1]
                    last = nc.vector.tensor_tensor(odd(permT[r, u * UT * P:(u + 1) * UT * P]), odd(LT[r, :]),
                                                   top.broadcast_to([64, UT * 4, T]), ALU.is_equal)
                last.then_inc(perm_done, 1)

            def save_one_hot(c, u, half):
                n = c * UNITS + u
                wait(dve, pbt_ready, n + 1)
                wait(dve, sel_ready, n * 8 - 4 + 4 * half)
                for j in (2, 3):
                    r = slice(32 * j, 32 * j + 32)
                    src = bank[3][r, half * 2 * P:(half + 1) * 2 * P].rearrange("p (t e) -> p t e", t=2)
                    last = nc.vector.tensor_copy(permBD[r, half, :, j, :], src)
                last.then_inc(pbd_dve, 1)

            def save_selected(c, u, m):
                n = c * UNITS + u
                wait(dve, sel_ready, n * 8 + m + 1)
                if u == 0 and m == 0:
                    wait(dve, sc_ready, c * (CT // 2))
                t, k = divmod(m, 2)
                copy_selected(nc.vector.tensor_copy, u, t, k, bank[4 + m % 4]).then_inc(sel_dve, 1)

            def chunk(c):
                chain[0], chain[1] = c * (UNITS * 7) + base, 0
                norm_unit(c, 0)
                one_hot(c, 0)
                save_one_hot(c, 0, 0)
                save_one_hot(c, 0, 1)
                norm_unit(c, 1)
                for u in range(UNITS):
                    for m in (0, 2):
                        save_selected(c, u, m)
                    if u + 1 < UNITS:
                        one_hot(c, u + 1)
                    for m in (4, 6):
                        save_selected(c, u, m)
                    if u + 1 < UNITS:
                        save_one_hot(c, u + 1, 0)
                        save_one_hot(c, u + 1, 1)
                    if u + 2 < UNITS:
                        norm_unit(c, u + 2)
                assert chain[1] == UNITS * 7
                for i in (1, 3):
                    wait(dve, in_ready, c * 4 + i + 1)
                    nc.vector.tensor_scalar(inner[:, 4 * i:4 * i + 4, :], bank[i][:, :], 0.0, None, ALU.max)\
                        .then_inc(in_dve, 1)
                for q in range(QUADS):
                    wait(dve, f2_ready, (c * QUADS + q) * 2 + 1)
                    wait(dve, moved[q % 2], (c * (QUADS // 2) + q // 2) * 16)
                    nc.vector.tensor_copy(stage[:, q % 2, 0:2, :], bank[4 + 2 * (q % 2)][:, :]).then_inc(st_dve, 1)
                for s in range(CT // 2):
                    n = c * (CT // 2) + s
                    wait(dve, sc_ready, n + 1)
                    xb = X1[:, 2 * n:2 * n + 2, :] if isinstance(n, int) else X1[:, bass.ds(n * 2, 2), :]
                    nc.vector.tensor_tensor(xb, xb, bank[s % 4][:, :].rearrange("p (t d) -> p t d", t=2), ALU.add)\
                        .then_inc(fin_done, 1)
            dve.wait_ge(zeroed, 4 + T)
            chunk(0)
            with dve.Fori(1, CHUNKS) as c:
                chunk(c)

    return nc


_INS = ['x', 'adj', 'L0_gnn_Wq', 'L0_gnn_bq', 'L0_gnn_Wk', 'L0_gnn_bk', 'L0_gnn_Wv', 'L0_gnn_bv', 'L0_gnn_Wo',
        'L0_gnn_bo', 'L0_ffn_controller', 'L0_ffn_f1', 'L0_ffn_f2']


def kernel(**inputs):
    import concourse.bacc as _bacc
    from concourse.bass_utils import run_bass_kernel_spmd as _run

    nc = _bacc.Bacc("TRN2", target_bir_lowering=False, num_devices=1)
    arrays, args = {}, []
    for name in _INS:
        a = np.ascontiguousarray(inputs[name])
        arrays[f"in_{name}"] = a
        args.append(nc.dram_tensor(f"in_{name}", a.shape, mybir.dt.from_np(a.dtype), kind="ExternalInput").ap())
    shape = inputs['x'].shape
    args.append(nc.dram_tensor("out_0", shape, F32, kind="ExternalOutput").ap())
    gnn_moe_kernel(nc, *args)
    r = _run(nc, [arrays], core_ids=[0])
    return r.results[0]["out_0"]
```

```python
from contextlib import ExitStack

import numpy as np

import concourse.bass as bass
from concourse import mybir

F32 = mybir.dt.float32
BF16 = mybir.dt.bfloat16
I32 = mybir.dt.int32
ALU = mybir.AluOpType
ACT = mybir.ActivationFunctionType
AX = mybir.AxisListType

P = 128
HEADS = 8
EPS = 1e-5
MASKED = -3.0e38
T = 16


def gnn_moe_kernel(nc, x, adj, Wq, bq, Wk, bk, Wv, bv, Wo, bo, controller, f1, f2, out):
    B, N, D = x.shape
    DH = D // HEADS
    KT = D // P
    QT = N // P
    G = HEADS * DH // P
    HPG = P // DH
    PAIRS = HEADS // 2
    SCALE = float(1.0 / np.sqrt(DH))
    TILES = B * N // P
    ES = controller.shape[1] * controller.shape[2]
    F = f1.shape[3]
    CT = 16
    CHUNKS = TILES // CT
    UT = 4
    UNITS = CT // UT
    GPT = P // T
    CG = CT * GPT
    CP = CG // 2
    QUADS = ES // 4
    assert D == 2 * P and N == 2 * P and DH == 32 and ES == 64 and F == 32 and CG == P and B % 4 == 0

    scratch = nc.dram_tensor("scratch", (CHUNKS * CG, ES * D), F32, kind="Internal").ap()

    def by_group(c, q, j):
        rows = slice(c * CG, c * CG + CG) if isinstance(c, int) else bass.ds(c * CG, CG)
        return scratch[rows, (4 * q + j) * D:(4 * q + j + 1) * D].rearrange("(b g) d -> g b d", g=32)

    def by_expert(c, tile):
        first = c * CG + GPT * tile
        rows = slice(first, first + GPT) if isinstance(c, int) else bass.ds(first, GPT)
        return scratch[rows, :].rearrange("(c two) (e d) -> (two e) c d", two=2, d=D)

    xt = x.rearrange("b (t p) d -> p (b t) d", p=P)
    ot = out.rearrange("b (t p) d -> p (b t) d", p=P)

    with ExitStack() as ctx:
        def sb(name, shape, dt=F32):
            return ctx.enter_context(nc.sbuf_tensor(name, shape, dt))

        def sem(name):
            return ctx.enter_context(nc.semaphore(name))

        X1 = sb("X1", [P, TILES, D])
        f1s = sb("f1s", [P, KT, ES, F])
        f2s = sb("f2s", [P, QUADS, D])
        ctl = sb("ctl", [P, KT, 2, ES])
        tie = sb("tie", [P, 1, T])
        ident = sb("ident", [P, P])
        identb = sb("identb", [P, P], BF16)
        stats = sb("stats", [P, 2, 6])
        mv = sb("mv", [P, QT, 2])
        mvr = sb("mvr", [P, QT, 2])
        mv2 = sb("mv2", [P, TILES, 2])
        root = sb("root", [P, 4, TILES])
        gmax = sb("gmax", [P, UT * GPT])

        region = sb("region", [P, KT * ES * CG])
        at = [0]

        def part(*shape):
            n = int(np.prod(shape))
            v = region[:, at[0]:at[0] + n]
            at[0] += n
            names = "abcd"[:len(shape)]
            if len(shape) > 1:
                v = v.rearrange(f"p ({' '.join(names)}) -> p {' '.join(names)}",
                                **{k: s for k, s in zip(names, shape)})
            return v

        KPad = part(2, G, HPG, N)
        PTs = part(HEADS, QT * N)
        Ps = part(2, QT, 2, N)
        WT = part(4, KT, D)
        QTs = part(2, G, N)
        Vs = part(2, QT, D)
        hT = part(KT, N)
        rexp = part(QT, D)
        rbc = part(G, N)
        bqs = part(G)
        bks = part(G)
        nmax = part(2, QT, 2)
        sums = part(HEADS, QT)
        rsum = part(HEADS, QT)
        nanv = part(2, QT)
        assert at[0] <= KT * ES * CG
        XS = region[:, :].rearrange("p (k e g) -> p k e g", k=KT, e=ES)

        h2 = sb("work", [P, 2, UT, D])
        hn = h2[:, 0, 0:QT, :]
        OT = h2[:, 0, 2:2 + G, :]
        wtmp = h2[:, 1, :, :]
        wtmp2 = h2[:, 0, :, :]
        h2T = sb("h2T", [P, KT, UT * P])
        LT = h2T[:, 0, :]
        one = sb("one", [P, 2, UT * P])
        permT = sb("permT", [P, CT * P])
        permBD = sb("permBD", [P, 2, 2, 4, P])
        innerBD = sb("innerBD", [P, 2, 4, 4, 32])
        stage = sb("stage", [P, 2, 4, D])
        XR = stage
        bvb = stage[:, 0, 0:2, :]
        bob = stage[:, 0, 2:4, :]
        maskb = stage[:, 1, 0:2, :].bitcast(BF16).rearrange("p a (b k) -> p a b k", b=2)

        adjs = permT[:, 0:QT * N].bitcast(I32).rearrange("p (t k) -> p t k", t=QT)
        adjf = permT[:, 512:512 + QT * N].rearrange("p (t k) -> p t k", t=QT)

        bank = [ctx.enter_context(nc.psum_tensor(f"bank{i}", [P, 512], F32)) for i in range(8)]
        S = bank[0:3]
        PTb = bank[4:6]
        Ob = bank[6]
        M = (bank[7], bank[3])

        w_in = sem("w_in")
        ffn_in = sem("ffn_in")
        x_in = [sem("x_in0"), sem("x_in1")]
        consts = sem("consts")
        zeroed = sem("zeroed")
        setup_dve = sem("setup_dve")
        wt_ready = sem("wt_ready")
        wt_saved = sem("wt_saved")
        dve_chain = sem("dve_chain")
        act_chain = sem("act_chain")
        ln_done = sem("ln_done")
        bo_added = sem("bo_added")
        hT_ready, hT_saved = sem("hT_ready"), sem("hT_saved")
        q_ready, q_saved = sem("q_ready"), sem("q_saved")
        k_ready, k_saved = sem("k_ready"), sem("k_saved")
        v_ready, v_saved = sem("v_ready"), sem("v_saved")
        s_ready = sem("s_ready")
        max_done = sem("max_done")
        exp_done = sem("exp_done")
        pt_ready = sem("pt_ready")
        pt_dve = sem("pt_dve")
        pt_act = sem("pt_act")
        pv_ready = sem("pv_ready")
        rexp_done = sem("rexp_done")
        rbc_ready, rbc_saved = sem("rbc_ready"), sem("rbc_saved")
        onorm_done = sem("onorm_done")
        wo_ready = sem("wo_ready")
        res_done = sem("res_done")
        h2_done = sem("h2_done")
        h2T_ready, h2T_saved = sem("h2T_ready"), sem("h2T_saved")
        log_ready, perm_done = sem("log_ready"), sem("perm_done")
        pbt_ready = sem("pbt_ready")
        pbd_dve, pbd_act = sem("pbd_dve"), sem("pbd_act")
        sel_ready = sem("sel_ready")
        sel_dve, sel_act = sem("sel_dve"), sem("sel_act")
        kept = sem("kept")
        in_ready = sem("in_ready")
        in_dve, in_act = sem("in_dve"), sem("in_act")
        f2_ready = sem("f2_ready")
        st_dve, st_act = sem("st_dve"), sem("st_act")
        moved = [sem("moved0"), sem("moved1")]
        gathered = [sem("gathered0"), sem("gathered1")]
        sc_ready = sem("sc_ready")
        fin_done = sem("fin_done")
        out_done = sem("out_done")

        block = ctx.enter_context(nc.Block())

        def wait(eng, s, value):
            if isinstance(value, int) and value <= 0:
                return
            eng.wait_ge(s, value)

        def batches(eng, body):
            body(0, 0, False)
            body(1, 1, False)
            with eng.Fori(1, B // 2 - 1) as i:
                for par in range(2):
                    body(i * 2 + par, par, False)
            body(B - 2, 0, False)
            body(B - 1, 1, True)

        def prev(b):
            return b - 1

        def copy_selected(copy, u, m):
            t, k = divmod(m, 2)
            tile = u * UT + t
            src = bank[4 + (8 * u + m) % 3][:, :].rearrange("p (g e) -> p g e", e=ES)
            return copy(XS[:, k, :, GPT * tile:GPT * tile + GPT].rearrange("p e g -> p g e"), src)

        def one_hot_block(half, j):
            r = slice(32 * j, 32 * j + 32)
            return (permBD[r, half, :, j, :],
                    bank[3][r, half * 2 * P:(half + 1) * 2 * P].rearrange("p (t e) -> p t e", t=2))

        def inner_block(q, j):
            r = slice(32 * j, 32 * j + 32)
            return innerBD[r, q % 2, :, j, :], bank[q % 2][r, 0:CG].rearrange("p (g i) -> p g i", g=4)

        @block.sync
        def _(sp):
            for k, W in enumerate((Wq, Wk)):
                sp.dma_start(wtmp[:, 2 * k:2 * k + 2, :], W.rearrange("(t p) i -> p t i", p=P)).then_inc(w_in, 16)
            for k, W in enumerate((Wv, Wo)):
                sp.dma_start(wtmp2[:, 2 * k:2 * k + 2, :], W.rearrange("(t p) i -> p t i", p=P)).then_inc(w_in, 16)
            sp.dma_start(adjs, adj.rearrange("(t p) k -> p t k", p=P)).then_inc(w_in, 16)
            sp.dma_start(X1[:, 0:QT, :], xt[:, 0:QT, :]).then_inc(x_in[0], 16)
            sp.dma_start(X1[:, QT:2 * QT, :], xt[:, QT:2 * QT, :]).then_inc(x_in[1], 16)
            with sp.Fori(1, B // 2) as i:
                for par in range(2):
                    sp.wait_ge(x_in[par], i * 16)
                    b = i * 2 + par
                    sp.dma_start(X1[:, bass.ds(b * QT, QT), :], xt[:, bass.ds(b * QT, QT), :]).then_inc(x_in[par], 16)
            sp.dma_start(f1s[:, :, :, :], f1.rearrange("(t p) e s f -> p t (e s) f", p=P)).then_inc(ffn_in, 16)
            for half in range(2):
                sp.dma_start(ctl[:, :, half, :], controller.rearrange("(t p) e s -> p t (e s)", p=P)).then_inc(ffn_in, 16)

            sp.dma_start(f2s[:, :, :], f2.rearrange("e s f d -> (e s f) d").rearrange("(q p) d -> p q d", p=P))\
              .then_inc(ffn_in, 16)
            def move(c, q):
                n = c * QUADS + q
                wait(sp, st_dve, n + 1)
                wait(sp, st_act, n + 1)
                for j in range(4):
                    sp.dma_start(by_group(c, q, j), stage[32 * j:32 * j + 32, q % 2, :, :]).then_inc(moved[q % 2], 16)

            def gather(c, tile):
                if tile < 2:
                    for m in moved:
                        wait(sp, m, (c + 1) * (QUADS // 2) * 64)
                else:
                    wait(sp, sc_ready, c * (CT // 2) + tile // 2)
                sp.dma_start(XR[:, tile % 2, :, :], by_expert(c, tile)).then_inc(gathered[tile % 2], 16)

            def store(c, s):
                n = c * (CT // 2) + s
                wait(sp, fin_done, n + 1)
                tiles = slice(2 * n, 2 * n + 2) if isinstance(n, int) else bass.ds(n * 2, 2)
                sp.dma_start(ot[:, tiles, :], X1[:, tiles, :]).then_inc(out_done, 16)

            with sp.Fori(0, CHUNKS) as c:
                for q in range(QUADS):
                    move(c, q)
                for s in range(CT // 2):
                    gather(c, 2 * s)
                    gather(c, 2 * s + 1)
                    if s > 0:
                        store(c, s - 1)
                store(c, CT // 2 - 1)
            sp.wait_ge(out_done, CHUNKS * (CT // 2) * 16)

        @block.gpsimd
        def _(pool):
            nc.gpsimd.memset(ident[:, :], 0.0).then_inc(consts, 1)
            nc.gpsimd.memset(identb[:, :], 0.0).then_inc(consts, 1)
            pool.wait_ge(consts, 2)
            for m in (ident, identb):
                nc.gpsimd.affine_select(out=m[:, :], in_=m[:, :], compare_op=ALU.not_equal, fill=1.0, base=0,
                                        pattern=[[-1, P]], channel_multiplier=1).then_inc(consts, 1)
            nc.gpsimd.memset(KPad, 0.0).then_inc(zeroed, 1)
            nc.gpsimd.memset(permBD[:, :, :, :, :], 0.0).then_inc(zeroed, 1)
            nc.gpsimd.memset(innerBD[:, :, :, :, :], 0.0).then_inc(zeroed, 1)
            nc.gpsimd.memset(one[:, :, :], 0.0).then_inc(zeroed, 1)
            values = np.linspace(0.0, 1e-6, T).astype(np.float32)
            for t in range(T):
                nc.gpsimd.memset(tie[:, 0, t:t + 1], float(values[t])).then_inc(zeroed, 1)

            pool.wait_ge(w_in, 16 * 9)

            def add_bo(b, par, last):
                wait(pool, ln_done, b + 1)
                xb = X1[:, bass.ds(b * QT, QT), :] if not isinstance(b, int) else X1[:, b * QT:b * QT + QT, :]
                nc.gpsimd.tensor_tensor(xb, xb, bob[:, :, :], ALU.add).then_inc(bo_added, 1)
            batches(pool, add_bo)

            def keep(c, u):
                n = c * UNITS + u
                wait(pool, perm_done, n + 1)
                wait(pool, sc_ready, (c - 1) * (CT // 2) + 2 * u + 2)
                nc.gpsimd.tensor_tensor(permT[:, u * UT * P:(u + 1) * UT * P], one[:, u % 2, :], one[:, u % 2, :],
                                        ALU.mult).then_inc(kept, 1)
            for u in range(UNITS):
                keep(0, u)
            with pool.Fori(1, CHUNKS) as c:
                for u in range(UNITS):
                    keep(c, u)

        @block.tensor
        def _(pe):
            pe.wait_ge(consts, 4)
            pe.wait_ge(w_in, 16 * 9)
            for k in range(4):
                src = wtmp if k < 2 else wtmp2
                for ob in range(KT):
                    for ib in range(KT):
                        last = nc.tensor.transpose(bank[k][:, ib * D + ob * P:ib * D + ob * P + P],
                                                   src[:, 2 * (k % 2) + ob, ib * P:ib * P + P], ident[:, :])
                last.then_inc(wt_ready, 1)
            pe.wait_ge(wt_saved, 4)

            def h_transpose(b):
                wait(pe, ln_done, b + 1)
                wait(pe, v_saved, b)
                for t in range(QT):
                    for k in range(KT):
                        last = nc.tensor.transpose(M[1][:, k * N + t * P:k * N + t * P + P],
                                                   hn[:, t, k * P:k * P + P], ident[:, :])
                last.then_inc(hT_ready, 1)

            def project(w, m, ready):
                for g in range(G):
                    for k in range(KT):
                        last = nc.tensor.matmul(m[:, g * N:g * N + N], WT[:, w, k, g * P:g * P + P], hT[:, k, :],
                                                start=(k == 0), stop=(k == KT - 1))
                last.then_inc(ready, 1)

            def q_project(b):
                wait(pe, hT_saved, b + 1)
                project(0, M[1], q_ready)

            def k_project(b):
                wait(pe, res_done, b - 1)
                project(1, M[0], k_ready)

            def v_project(b):
                wait(pe, q_saved, b + 1)
                for t in range(QT):
                    for k in range(KT):
                        last = nc.tensor.matmul(M[1][:, t * D:t * D + D], hT[:, k, t * P:t * P + P], WT[:, 2, k, :],
                                                start=(k == 0), stop=(k == KT - 1))
                last.then_inc(v_ready, 1)

            def scores(b, par, pr):
                g, j = divmod(2 * pr, HPG)
                if pr == 0:
                    wait(pe, q_saved, b + 1)
                    wait(pe, k_saved, b + 1)
                for t in range(QT):
                    n = 2 * pr + t
                    before = n - 3 if n > 2 else (-2, -1, -3)[n]
                    wait(pe, exp_done, b * 8 + before + 1)
                    s = S[n % 3]
                    nc.tensor.matmul(s[:, :], identb[:, :], maskb[:, t, :, :], start=True, stop=False)
                    nc.tensor.matmul(s[:, :], QTs[:, par, g, t * P:t * P + P], KPad[:, par, g, j:j + 2, :],
                                     start=False, stop=True).then_inc(s_ready, 1)

            def p_transpose(b, par, pr):
                wait(pe, exp_done, b * 8 + 2 * pr + 2)
                for h in (2 * pr, 2 * pr + 1):
                    o = h - 2
                    bb, o = (b, o) if o >= 0 else (prev(b), o + 8)
                    if o % 4 == 3:
                        wait(pe, pt_act, bb * 2 + o // 4 + 1)
                    else:
                        wait(pe, pt_dve, bb * 6 + (o // 4) * 3 + o % 4 + 1)
                    for k in range(QT):
                        for t in range(QT):
                            last = nc.tensor.transpose(PTb[h % 2][:, k * N + t * P:k * N + t * P + P],
                                                       Ps[:, pr % 2, t, h % 2, k * P:k * P + P], ident[:, :])
                    last.then_inc(pt_ready, 1)

            def pv(b, par, g):
                wait(pe, pt_dve, b * 6 + 3 * g + 3)
                wait(pe, pt_act, b * 2 + g + 1)
                if g == 0:
                    wait(pe, onorm_done, b)
                    wait(pe, v_saved, b + 1)
                for k in range(QT):
                    for j in range(HPG):
                        h = g * HPG + j
                        last = nc.tensor.matmul(Ob[32 * j:32 * j + 32, g * N:g * N + N],
                                                Vs[:, par, k, h * DH:h * DH + DH], PTs[:, h, k * N:k * N + N],
                                                start=(k == 0), stop=(k == QT - 1))
                last.then_inc(pv_ready, 1)

            def r_transpose(b, last):
                wait(pe, rexp_done, b + 1)
                if not last:
                    wait(pe, k_saved, b + 2)
                for g in range(G):
                    for t in range(QT):
                        last = nc.tensor.transpose(M[0][:, g * N + t * P:g * N + t * P + P],
                                                   rexp[:, t, g * P:g * P + P], ident[:, :])
                last.then_inc(rbc_ready, 1)

            def o_project(b):
                wait(pe, onorm_done, b + 1)
                wait(pe, rbc_saved, b + 1)
                for t in range(QT):
                    for g in range(G):
                        last = nc.tensor.matmul(M[0][:, t * D:t * D + D], OT[:, g, t * P:t * P + P], WT[:, 3, g, :],
                                                start=(g == 0), stop=(g == G - 1))
                last.then_inc(wo_ready, 1)

            h_transpose(0)
            q_project(0)
            k_project(0)

            def batch(b, par, last):
                first = isinstance(b, int) and b == 0
                scores(b, par, 0)
                v_project(b)
                if not first:
                    pv(prev(b), 1 - par, 1)
                scores(b, par, 1)
                if not first:
                    r_transpose(prev(b), False)
                p_transpose(b, par, 0)
                scores(b, par, 2)
                if not last:
                    h_transpose(b + 1)
                p_transpose(b, par, 1)
                if not first:
                    o_project(prev(b))
                scores(b, par, 3)
                if not last:
                    q_project(b + 1)
                p_transpose(b, par, 2)
                if not last:
                    k_project(b + 1)
                pv(b, par, 0)
                p_transpose(b, par, 3)
            batches(pe, batch)
            pv(B - 1, 1, 1)
            r_transpose(B - 1, True)
            o_project(B - 1)

            pe.wait_ge(ffn_in, 16 * 4)
            pe.wait_ge(zeroed, 4 + T)
            pe.wait_ge(res_done, B)

            def unit_transpose(n, par):
                wait(pe, h2_done, n + 1)
                for k in range(KT):
                    for t in range(UT):
                        last = nc.tensor.transpose(bank[k][:, t * P:t * P + P],
                                                   h2[:, par, t, k * P:k * P + P], ident[:, :])
                last.then_inc(h2T_ready, 1)

            def logits(n):
                wait(pe, h2T_saved, n + 1)
                wait(pe, perm_done, n)
                for k in range(KT):
                    last = nc.tensor.matmul(bank[2][:, :], ctl[:, k, :, :], h2T[:, k, :],
                                            start=(k == 0), stop=(k == KT - 1))
                last.then_inc(log_ready, 1)

            def one_hot_transpose(n, par):
                wait(pe, perm_done, n + 1)
                wait(pe, pbd_dve, 2 * n)
                wait(pe, pbd_act, 2 * n)
                for t in range(UT):
                    last = nc.tensor.transpose(bank[3][:, t * P:t * P + P],
                                               one[:, par, t * P:t * P + P], ident[:, :])
                last.then_inc(pbt_ready, 1)

            def select(c, u, t):
                n = c * UNITS + u
                half = t // 2
                wait(pe, pbd_dve, 2 * n + half + 1)
                wait(pe, pbd_act, 2 * n + half + 1)
                for k in range(KT):
                    m = 8 * u + 2 * t + k
                    if m >= 3:
                        o = m - 3
                        wait(pe, sel_act if o % 2 else sel_dve, c * 4 * UNITS + o // 2 + 1)
                    elif m == 0:
                        wait(pe, st_dve, c * QUADS)
                        wait(pe, st_act, c * QUADS)
                    nc.tensor.matmul(bank[4 + m % 3][:, :], h2[:, u % 2, t, k * P:k * P + P],
                                     permBD[:, half, t % 2, :, :], start=True, stop=True).then_inc(sel_ready, 1)

            def expand(c, q):
                n = c * QUADS + q
                if q > 1:
                    wait(pe, in_dve, n - 1)
                    wait(pe, in_act, n - 1)
                for k in range(KT):
                    for j in range(4):
                        last = nc.tensor.matmul(bank[q % 2][32 * j:32 * j + 32, 0:CG],
                                                f1s[:, k, 4 * q + j, :], XS[:, k, 4 * q + j, :],
                                                start=(k == 0), stop=(k == KT - 1))
                last.then_inc(in_ready, 1)

            def contract(c, q):
                n = c * QUADS + q
                wait(pe, in_dve, n + 1)
                wait(pe, in_act, n + 1)
                for hf in range(2):
                    if q > 1:
                        wait(pe, st_act if hf else st_dve, n - 1)
                    for g in (2 * hf, 2 * hf + 1):
                        last = nc.tensor.matmul(bank[4 + 2 * (q % 2) + hf][:, g % 2 * D:g % 2 * D + D],
                                                innerBD[:, q % 2, g, :, :], f2s[:, q, :], start=True, stop=True)
                    last.then_inc(f2_ready, 1)

            def scatter(c, s):
                n = c * (CT // 2) + s
                if s == 0:
                    wait(pe, kept, (c + 1) * UNITS)
                if s > 0:
                    wait(pe, fin_done, n)
                for tt in range(2):
                    wait(pe, gathered[tt], (n + 1) * 16)
                    for j in range(4):
                        pr = (2 * s + tt) * 4 + j
                        last = nc.tensor.matmul(bank[7][32 * j:32 * j + 32, tt * D:tt * D + D],
                                                permT[:, pr * 32:pr * 32 + 32], XR[:, tt, j, :],
                                                start=True, stop=True)
                last.then_inc(sc_ready, 1)

            def unit(c, u, front, back):
                n = c * UNITS + u + 1
                select(c, u, 0)
                if front:
                    unit_transpose(n, (u + 1) % 2)
                select(c, u, 1)
                if front:
                    logits(n)
                if back:
                    scatter(c - 1, 2 * u)
                select(c, u, 2)
                if front:
                    one_hot_transpose(n, (u + 1) % 2)
                select(c, u, 3)
                if back:
                    scatter(c - 1, 2 * u + 1)

            def experts(c):
                pe.wait_ge(sel_dve, (c + 1) * UNITS * 4)
                pe.wait_ge(sel_act, (c + 1) * UNITS * 4)
                expand(c, 0)
                for q in range(QUADS):
                    if q + 1 < QUADS:
                        expand(c, q + 1)
                    contract(c, q)

            unit_transpose(0, 0)
            logits(0)
            one_hot_transpose(0, 0)
            for u in range(UNITS):
                unit(0, u, True, False)
            experts(0)
            with pe.Fori(1, CHUNKS - 1) as c:
                for u in range(UNITS):
                    unit(c, u, True, True)
                experts(c)
            for u in range(UNITS):
                unit(CHUNKS - 1, u, u + 1 < UNITS, True)
            experts(CHUNKS - 1)
            for s in range(CT // 2):
                scatter(CHUNKS - 1, s)

        @block.scalar
        def _(act):
            for t, b in ((bqs, bq), (bks, bk)):
                act.dma_start(t[:, :], b.rearrange("(g p) -> p g", p=P), allow_slow_non_contiguous=True).then_inc(w_in, 16)
            act.dma_start(bvb[:, :, :], bv.partition_broadcast(P).unsqueeze(1).broadcast_to([P, 2, D])).then_inc(w_in, 16)
            act.dma_start(bob[:, :, :], bo.partition_broadcast(P).unsqueeze(1).broadcast_to([P, 2, D])).then_inc(w_in, 16)
            act.wait_ge(w_in, 16 * 9)
            nc.scalar.mul(bqs[:, :], bqs[:, :], SCALE).then_inc(act_chain, 1)
            for k in range(4):
                act.wait_ge(wt_ready, k + 1)
                nc.scalar.copy(WT[:, k, :, :], bank[k][:, :]).then_inc(wt_saved, 1)
            act.wait_ge(act_chain, 1)
            act.wait_ge(zeroed, 1)

            def save_hT(b):
                wait(act, hT_ready, b + 1)
                nc.scalar.copy(hT, M[1][:, :]).then_inc(hT_saved, 1)

            def save_q(b, par):
                wait(act, q_ready, b + 1)
                for g in range(G):
                    last = nc.scalar.activation(QTs[:, par, g, :], M[1][:, g * N:g * N + N], ACT.Identity,
                                                bias=bqs[:, g:g + 1], scale=SCALE)
                last.then_inc(q_saved, 1)

            def save_k(b, par):
                wait(act, k_ready, b + 1)
                for g in range(G):
                    for j in range(HPG):
                        r = slice(32 * j, 32 * j + 32)
                        last = nc.scalar.activation(KPad[r, par, g, j, :], M[0][r, g * N:g * N + N], ACT.Identity,
                                                    bias=bks[r, g:g + 1])
                last.then_inc(k_saved, 1)

            def exps(b, pr):
                if pr < 2:
                    wait(act, pt_ready, b * 8 + 4 * (pr // 2) + 2 * pr - 2)
                else:
                    wait(act, pt_ready, b * 8 + 2 * (pr - 2) + 2)
                if pr == 0:
                    wait(act, rexp_done, b)
                for t in range(QT):
                    wait(act, max_done, b * 8 + 2 * pr + t + 1)
                    for h in range(2):
                        last = nc.scalar.activation(Ps[:, pr % 2, t, h, :], S[(2 * pr + t) % 3][:, h * N:h * N + N],
                                                    ACT.Exp, bias=nmax[:, pr % 2, t, h:h + 1],
                                                    accum_out=sums[:, 2 * pr + h, t:t + 1])
                    last.then_inc(exp_done, 1)

            def save_pt(b, h):
                wait(act, pt_ready, b * 8 + h + 1)
                wait(act, pv_ready, 2 * b + h // 4 - 1)
                nc.scalar.copy(PTs[:, h, :], PTb[h % 2][:, :]).then_inc(pt_act, 1)

            def save_rbc(b):
                wait(act, rbc_ready, b + 1)
                nc.scalar.copy(rbc, M[0][:, :]).then_inc(rbc_saved, 1)

            save_hT(0)
            save_q(0, 0)
            save_k(0, 0)

            def batch(b, par, last):
                first = isinstance(b, int) and b == 0
                if not first:
                    save_pt(prev(b), 7)
                exps(b, 0)
                exps(b, 1)
                if not first:
                    save_rbc(prev(b))
                exps(b, 2)
                if not last:
                    save_hT(b + 1)
                save_pt(b, 3)
                exps(b, 3)
                if not last:
                    save_q(b + 1, 1 - par)
                    save_k(b + 1, 1 - par)
            batches(act, batch)
            save_pt(B - 1, 7)
            save_rbc(B - 1)

            def save_h2T(n):
                wait(act, h2T_ready, n + 1)
                wait(act, perm_done, n)
                for k in range(KT):
                    last = nc.scalar.copy(h2T[:, k, :], bank[k][:, :])
                last.then_inc(h2T_saved, 1)

            def save_one_hot(n, half):
                wait(act, pbt_ready, n + 1)
                wait(act, sel_ready, n * 8 - 4 + 4 * half)
                for j in (0, 1):
                    last = nc.scalar.copy(*one_hot_block(half, j))
                last.then_inc(pbd_act, 1)

            def save_selected(c, u, m):
                wait(act, sel_ready, (c * UNITS + u) * 8 + m + 1)
                copy_selected(nc.scalar.copy, u, m).then_inc(sel_act, 1)

            def unit(c, u, front):
                n = c * UNITS + u + 1
                save_selected(c, u, 1)
                if front:
                    save_h2T(n)
                save_selected(c, u, 3)
                save_selected(c, u, 5)
                if front:
                    save_one_hot(n, 0)
                save_selected(c, u, 7)
                if front:
                    save_one_hot(n, 1)

            def experts(c):
                def save_inner(q):
                    wait(act, in_ready, c * QUADS + q + 1)
                    wait(act, f2_ready, (c * QUADS + q) * 2 - 2)
                    for j in (0, 1):
                        dst, src = inner_block(q, j)
                        last = nc.scalar.activation(dst, src, ACT.Relu)
                    last.then_inc(in_act, 1)
                save_inner(0)
                for q in range(QUADS):
                    if q + 1 < QUADS:
                        save_inner(q + 1)
                    wait(act, f2_ready, (c * QUADS + q) * 2 + 2)
                    wait(act, moved[q % 2], (c * (QUADS // 2) + q // 2) * 64)
                    nc.scalar.copy(stage[:, q % 2, 2:4, :], bank[5 + 2 * (q % 2)][:, :]).then_inc(st_act, 1)

            act.wait_ge(zeroed, 4 + T)
            save_h2T(0)
            save_one_hot(0, 0)
            save_one_hot(0, 1)
            for u in range(UNITS):
                unit(0, u, True)
            experts(0)
            with act.Fori(1, CHUNKS - 1) as c:
                for u in range(UNITS):
                    unit(c, u, True)
                experts(c)
            for u in range(UNITS):
                unit(CHUNKS - 1, u, u + 1 < UNITS)
            experts(CHUNKS - 1)

        @block.vector
        def _(dve):
            chain = [0, 0]

            def link(ins):
                chain[1] += 1
                ins.then_inc(dve_chain, 1)
                dve.wait_ge(dve_chain, chain[0] + chain[1])

            dve.wait_ge(w_in, 16 * 9)
            link(nc.vector.tensor_scalar(adjf, adjs, 0, None, ALU.not_equal))
            link(nc.vector.tensor_reduce(nanv[:, 0, :], adjf, AX.X, ALU.max))
            link(nc.vector.reciprocal(nanv[:, 1, :], nanv[:, 0, :]))
            link(nc.vector.tensor_tensor(nanv[:, 1, :], nanv[:, 1, :], nanv[:, 0, :], ALU.mult))
            for h in range(2):
                last = nc.vector.tensor_scalar(maskb[:, :, h, :], adjf, 0.0, MASKED, ALU.is_equal, ALU.mult)
            last.then_inc(setup_dve, 1)
            dve.wait_ge(wt_ready, 4)

            def statistics(tile, dst):
                nc.vector.memset(root[:, 3, 0:1], 0.0)
                for t in range(QT):
                    last = nc.vector.bn_stats(stats[:, t, :], tile(t))
                link(last)
                nc.vector.memset(root[:, 3, 0:1], 0.0)
                for t in range(QT):
                    last = nc.vector.bn_aggr(dst(t), stats[:, t, :])
                return last

            def inverse_root(n, variance):
                X, Y, A, C = (root[:, i, 0:n] for i in range(4))
                link(nc.vector.tensor_scalar(X, variance, EPS, None, ALU.add))
                link(nc.vector.tensor_scalar(Y.bitcast(I32), X.bitcast(I32), -0.5, float(0x5f3759df),
                                             ALU.mult, ALU.add))
                for _ in range(3):
                    link(nc.vector.scalar_tensor_tensor(A, Y, -0.5, Y, ALU.mult, ALU.mult))
                    link(nc.vector.tensor_tensor(C, A, X, ALU.mult))
                    link(nc.vector.scalar_tensor_tensor(Y, C, 1.5, Y, ALU.add, ALU.mult))
            ROOT_LINKS = 11

            def xtile(i):
                return X1[:, i, :] if isinstance(i, int) else X1[:, bass.ds(i, 1), :].rearrange("p o d -> p (o d)")

            def xbatch(b):
                return X1[:, b * QT:b * QT + QT, :] if isinstance(b, int) else X1[:, bass.ds(b * QT, QT), :]

            def layer_norm(b, par):
                wait(dve, x_in[par], (b // 2) * 16 + 16 if isinstance(b, int) else (b - par) * 8 + 16)
                link(statistics(lambda t: xtile(b * QT + t), lambda t: mv[:, t, :]))
                inverse_root(QT, mv[:, :, 1])

            def apply_norm(b):
                wait(dve, hT_ready, b)
                for t in range(QT):
                    last = nc.vector.tensor_scalar(hn[:, t, :], xtile(b * QT + t), mv[:, t, 0:1],
                                                   root[:, 1, t:t + 1], ALU.subtract, ALU.mult)
                last.then_inc(ln_done, 1)

            def save_v(b, par):
                wait(dve, v_ready, b + 1)
                nc.vector.tensor_tensor(Vs[:, par, :, :], M[1][:, :].rearrange("p (t d) -> p t d", t=QT), bvb[:, :, :],
                                        ALU.add).then_inc(v_saved, 1)

            def maxima(b, pr):
                for t in range(QT):
                    n = 2 * pr + t
                    wait(dve, s_ready, b * 8 + n + 1)
                    wait(dve, exp_done, b * 8 + n - 3)
                    nc.vector.tensor_reduce(nmax[:, pr % 2, t, :], S[n % 3][:, :].rearrange("p (h k) -> p h k", h=2),
                                            AX.X, ALU.max, negate=True).then_inc(max_done, 1)

            def save_pt(b, h):
                wait(dve, pt_ready, b * 8 + h + 1)
                wait(dve, pv_ready, 2 * b + h // 4 - 1)
                nc.vector.tensor_copy(PTs[:, h, :], PTb[h % 2][:, :]).then_inc(pt_dve, 1)

            def reciprocals(b):
                wait(dve, exp_done, b * 8 + 8)
                link(nc.vector.reciprocal(rsum[:, :, :], sums[:, :, :]))
                for t in range(QT):
                    last = nc.vector.tensor_scalar(
                        rexp[:, t, :].rearrange("p (h d) -> p h d", h=HEADS),
                        rsum[:, :, t:t + 1].broadcast_to([P, HEADS, DH]), nanv[:, 1, t:t + 1], None, ALU.mult)
                last.then_inc(rexp_done, 1)

            def normalise(b):
                wait(dve, rbc_saved, b + 1)
                wait(dve, pv_ready, 2 * b + 2)
                nc.vector.tensor_tensor(OT, Ob[:, :].rearrange("p (g q) -> p g q", g=G), rbc, ALU.mult)\
                    .then_inc(onorm_done, 1)

            def residual(b):
                wait(dve, wo_ready, b + 1)
                wait(dve, bo_added, b + 1)
                xb = xbatch(b)
                nc.vector.tensor_tensor(xb, xb, M[0][:, :].rearrange("p (t d) -> p t d", t=QT), ALU.add)\
                    .then_inc(res_done, 1)
                wait(dve, res_done, b + 1)
                link(statistics(lambda t: xtile(b * QT + t), lambda t: mvr[:, t, :]))
                tiles = slice(b * QT, b * QT + QT) if isinstance(b, int) else bass.ds(b * QT, QT)
                nc.vector.tensor_copy(mv2[:, tiles, :], mvr[:, :, :])

            layer_norm(0, 0)
            apply_norm(0)
            layer_norm(1, 1)
            apply_norm(1)
            before = chain[1]
            FRONT = 2 + ROOT_LINKS
            BACK = 3
            LINKS = FRONT + BACK

            def batch(b, par, last):
                first = isinstance(b, int) and b == 0
                late = isinstance(b, int) and b >= B - 2
                chain[0], chain[1] = (before if first else b * LINKS + (before - BACK)), 0
                if last:
                    chain[0] -= FRONT
                if not first:
                    save_pt(prev(b), 6)
                    reciprocals(prev(b))
                maxima(b, 0)
                save_v(b, par)
                maxima(b, 1)
                if not first:
                    normalise(prev(b))
                save_pt(b, 0)
                save_pt(b, 1)
                maxima(b, 2)
                save_pt(b, 2)
                if not first:
                    residual(prev(b))
                maxima(b, 3)
                if not late:
                    layer_norm(b + 2, par)
                save_pt(b, 4)
                save_pt(b, 5)
                if not late:
                    apply_norm(b + 2)
            batches(dve, batch)
            chain[0], chain[1] = chain[0] + chain[1], 0
            save_pt(B - 1, 6)
            reciprocals(B - 1)
            normalise(B - 1)
            residual(B - 1)
            nc.vector.memset(rsum[:, :, :], 0.0).then_inc(dve_chain, 1)
            chain[1] += 1
            dve.wait_ge(dve_chain, chain[0] + chain[1])
            inverse_root(TILES, mv2[:, :, 1])
            base = chain[0] + chain[1]

            def norm_unit(n, par):
                wait(dve, sel_ready, n * 8 - 8)
                for t in range(UT):
                    tile = n * UT + t
                    if isinstance(n, int):
                        mean, r = mv2[:, tile, 0:1], root[:, 1, tile:tile + 1]
                    else:
                        mean = mv2[:, bass.ds(tile, 1), 0:1].rearrange("p a b -> p (a b)")
                        r = root[:, 1, bass.ds(tile, 1)]
                    last = nc.vector.tensor_scalar(h2[:, par, t, :], xtile(tile), mean, r, ALU.subtract, ALU.mult)
                last.then_inc(h2_done, 1)

            def one_hot(n, par):
                wait(dve, log_ready, n + 1)
                link(nc.vector.tensor_tensor(LT.rearrange("p (g t) -> p g t", t=T),
                                             bank[2][:, :].rearrange("p (g t) -> p g t", t=T),
                                             tie[:, :, :].broadcast_to([P, UT * GPT, T]), ALU.add))
                link(nc.vector.tensor_reduce(gmax[:, :], LT.rearrange("p (g t) -> p g t", t=T), AX.X, ALU.max))
                wait(dve, kept, n - 1)
                for half in range(2):
                    r = slice(64 * half, 64 * half + 64)

                    def own(v):
                        return v.rearrange("p (c two t) -> p c two t", two=2, t=T)[:, :, half, :]
                    top = gmax[r, :].rearrange("p (c two) -> p c two", two=2)[:, :, half:half + 1]
                    last = nc.vector.tensor_tensor(own(one[r, par, :]), own(LT[r, :]),
                                                   top.broadcast_to([64, UT * 4, T]), ALU.is_equal)
                last.then_inc(perm_done, 1)

            def save_one_hot(n, half):
                wait(dve, pbt_ready, n + 1)
                wait(dve, sel_ready, n * 8 - 4 + 4 * half)
                for j in (2, 3):
                    last = nc.vector.tensor_copy(*one_hot_block(half, j))
                last.then_inc(pbd_dve, 1)

            def save_selected(c, u, m):
                wait(dve, sel_ready, (c * UNITS + u) * 8 + m + 1)
                copy_selected(nc.vector.tensor_copy, u, m).then_inc(sel_dve, 1)

            def finish(c, s):
                n = c * (CT // 2) + s
                wait(dve, sc_ready, n + 1)
                xb = X1[:, 2 * n:2 * n + 2, :] if isinstance(n, int) else X1[:, bass.ds(n * 2, 2), :]
                nc.vector.tensor_tensor(xb, xb, bank[7][:, :].rearrange("p (t d) -> p t d", t=2), ALU.add)\
                    .then_inc(fin_done, 1)

            def unit(c, u, front, back):
                n = c * UNITS + u + 1
                chain[0], chain[1] = (n - 1) * 2 + base + 2, 0
                if front:
                    norm_unit(n, (u + 1) % 2)
                save_selected(c, u, 0)
                save_selected(c, u, 2)
                if front:
                    one_hot(n, (u + 1) % 2)
                save_selected(c, u, 4)
                if back:
                    finish(c - 1, 2 * u)
                if front:
                    save_one_hot(n, 0)
                save_selected(c, u, 6)
                if back:
                    finish(c - 1, 2 * u + 1)
                if front:
                    save_one_hot(n, 1)

            def experts(c):
                def save_inner(q):
                    wait(dve, in_ready, c * QUADS + q + 1)
                    wait(dve, f2_ready, (c * QUADS + q) * 2 - 2)
                    for j in (2, 3):
                        dst, src = inner_block(q, j)
                        last = nc.vector.tensor_scalar(dst, src, 0.0, None, ALU.max)
                    last.then_inc(in_dve, 1)
                save_inner(0)
                for q in range(QUADS):
                    if q + 1 < QUADS:
                        save_inner(q + 1)
                    wait(dve, f2_ready, (c * QUADS + q) * 2 + 1)
                    wait(dve, moved[q % 2], (c * (QUADS // 2) + q // 2) * 64)
                    nc.vector.tensor_copy(stage[:, q % 2, 0:2, :], bank[4 + 2 * (q % 2)][:, :]).then_inc(st_dve, 1)

            dve.wait_ge(zeroed, 4 + T)
            chain[0], chain[1] = base, 0
            norm_unit(0, 0)
            one_hot(0, 0)
            save_one_hot(0, 0)
            save_one_hot(0, 1)
            for u in range(UNITS):
                unit(0, u, True, False)
            experts(0)
            with dve.Fori(1, CHUNKS - 1) as c:
                for u in range(UNITS):
                    unit(c, u, True, True)
                experts(c)
            for u in range(UNITS):
                unit(CHUNKS - 1, u, u + 1 < UNITS, True)
            experts(CHUNKS - 1)
            for s in range(CT // 2):
                finish(CHUNKS - 1, s)

    return nc


_INS = ['x', 'adj', 'L0_gnn_Wq', 'L0_gnn_bq', 'L0_gnn_Wk', 'L0_gnn_bk', 'L0_gnn_Wv', 'L0_gnn_bv', 'L0_gnn_Wo',
        'L0_gnn_bo', 'L0_ffn_controller', 'L0_ffn_f1', 'L0_ffn_f2']


def kernel(**inputs):
    import concourse.bacc as _bacc
    from concourse.bass_utils import run_bass_kernel_spmd as _run

    nc = _bacc.Bacc("TRN2", target_bir_lowering=False, num_devices=1)
    arrays, args = {}, []
    for name in _INS:
        a = np.ascontiguousarray(inputs[name])
        arrays[f"in_{name}"] = a
        args.append(nc.dram_tensor(f"in_{name}", a.shape, mybir.dt.from_np(a.dtype), kind="ExternalInput").ap())
    shape = inputs['x'].shape
    args.append(nc.dram_tensor("out_0", shape, F32, kind="ExternalOutput").ap())
    gnn_moe_kernel(nc, *args)
    r = _run(nc, [arrays], core_ids=[0])
    return r.results[0]["out_0"]
```

```python
from contextlib import ExitStack

import numpy as np

import concourse.bass as bass
from concourse import mybir

F32 = mybir.dt.float32
F32R = mybir.dt.float32r
BF16 = mybir.dt.bfloat16
I32 = mybir.dt.int32
ALU = mybir.AluOpType
ACT = mybir.ActivationFunctionType
AX = mybir.AxisListType

P = 128
HEADS = 8
EPS = 1e-5
MASKED = -3.0e38
T = 16


def gnn_moe_kernel(nc, x, adj, Wq, bq, Wk, bk, Wv, bv, Wo, bo, controller, f1, f2, out):
    B, N, D = x.shape
    DH = D // HEADS
    KT = D // P
    QT = N // P
    G = HEADS * DH // P
    HPG = P // DH
    SCALE = float(1.0 / np.sqrt(DH))
    TILES = B * N // P
    ES = controller.shape[1] * controller.shape[2]
    F = f1.shape[3]
    CT = 16
    CHUNKS = TILES // CT
    UT = 4
    UNITS = CT // UT
    GPT = P // T
    CG = CT * GPT
    CP = CG // 2
    QUADS = ES // 4
    assert D == 2 * P and N == 2 * P and DH == 32 and ES == 64 and F == 32 and CG == P and B % 4 == 0

    scratch = nc.dram_tensor("scratch", (CHUNKS * CG, ES * D), F32, kind="Internal").ap()

    def by_group(c, q, j):
        rows = slice(c * CG, c * CG + CG) if isinstance(c, int) else bass.ds(c * CG, CG)
        return scratch[rows, (4 * q + j) * D:(4 * q + j + 1) * D].rearrange("(b g) d -> g b d", g=32)

    def by_expert(c, tile):
        first = c * CG + GPT * tile
        rows = slice(first, first + GPT) if isinstance(c, int) else bass.ds(first, GPT)
        return scratch[rows, :].rearrange("(c two) (e d) -> (two e) c d", two=2, d=D)

    xt = x.rearrange("b (t p) d -> p (b t) d", p=P)
    ot = out.rearrange("b (t p) d -> p (b t) d", p=P)

    with ExitStack() as ctx:
        def sb(name, shape, dt=F32):
            return ctx.enter_context(nc.sbuf_tensor(name, shape, dt))

        def sem(name):
            return ctx.enter_context(nc.semaphore(name))

        X1 = sb("X1", [P, TILES, D])
        f1s = sb("f1s", [P, KT, ES, F])
        f2s = sb("f2s", [P, QUADS, D])
        ctl = sb("ctl", [P, KT, 2, ES])
        tie = sb("tie", [P, 1, T])
        ident = sb("ident", [P, P])
        identb = sb("identb", [P, P], BF16)
        stats = sb("stats", [P, 2, 6])
        mv = sb("mv", [P, QT, 2])
        newt = sb("newt", [P, 1])
        mvr = sb("mvr", [P, QT, 2])
        mv2 = sb("mv2", [P, TILES, 2])
        root = sb("root", [P, 4, TILES])
        gmax = sb("gmax", [P, UT * GPT])

        few = sb("few", [P, 4, 2])
        bqs, bks, bvs = (few[:, i, :] for i in range(3))
        shift = few[:, 3, :]
        nmax = sb("nmax", [P, 2, QT, 2])
        sums = sb("sums", [P, HEADS, QT])
        rsum = sb("rsum", [P, HEADS, QT])
        nanv = sb("nanv", [P, 2, QT])

        floor = (nc.sbuf_base + 31) // 32 * 32
        at = [floor]

        def place(name, shape, dt=F32):
            v = nc.alloc_sbuf_tensor_at(name, shape, dt, offset=at[0])
            at[0] += int(np.prod(shape[1:])) * (2 if dt == BF16 else 4)
            return v

        parts = place("parts", [P, 4, G, N], F32R)
        stack = place("stack", [P, 2, HPG, 2, G * N], F32R)
        PTs = place("PTs", [P, HEADS, QT * N])
        Ps = place("Ps", [P, 2, QT, 2, N])
        WT = place("WT", [P, 4, KT, D])
        Vs = place("Vs", [P, 2, QT, D])
        hT = place("hT", [P, KT, N])
        rexp = place("rexp", [P, QT, D])
        rbc = place("rbc", [P, G, N])
        hn = place("hn", [P, QT, D])
        OT = place("OT", [P, G, N])
        bob = place("bob", [P, 2, D])
        maskb = place("maskb", [P, QT, 2, N], BF16)
        attention_end = at[0]
        bvx = Ps[:, 0, 0, :, 0:P]
        wtmp = PTs[:, 0:4, :].rearrange("p h (a d) -> p (h a) d", a=2)
        adjs = PTs[:, 4, :].bitcast(I32).rearrange("p (t k) -> p t k", t=QT)
        adjf = PTs[:, 5, :].rearrange("p (t k) -> p t k", t=QT)

        at[0] = floor
        XS = place("XS", [P, KT, ES, CG])
        h2 = place("h2", [P, 2, UT, D])
        h2T = place("h2T", [P, KT, UT * P])
        LT = h2T[:, 0, :]
        permT = place("permT", [P, CT * P])
        stage = place("stage", [P, 2, 4, D])
        XRlast = nc.alloc_sbuf_tensor_at("XRlast", [P, CT, 4, D], F32, offset=floor)
        XR = stage
        assert at[0] >= attention_end
        one = place("one", [P, 2, UT * P])
        permBD = place("permBD", [P, 2, 2, 4, P])
        innerBD = place("innerBD", [P, 2, 4, 4, 32])
        assert at[0] <= nc.sbuf_usable_end

        bank = [ctx.enter_context(nc.psum_tensor(f"bank{i}", [P, 512], F32)) for i in range(8)]
        S = bank[0:3]
        PTb = bank[4:6]
        Ob = bank[6]
        M = (bank[7], bank[3])

        w_in = sem("w_in")
        ffn_in = sem("ffn_in")
        x_in = [sem("x_in0"), sem("x_in1")]
        consts = sem("consts")
        zeroed = sem("zeroed")
        setup_dve = sem("setup_dve")
        wt_ready = sem("wt_ready")
        wt_saved = sem("wt_saved")
        dve_chain = sem("dve_chain")
        act_chain = sem("act_chain")
        ln_done = sem("ln_done")
        bo_added = sem("bo_added")
        bias_ready, bias_done = sem("bias_ready"), sem("bias_done")
        root_done = sem("root_done")
        last_in = [sem(f"last_in{i}") for i in range(4)]
        hT_ready, hT_saved = sem("hT_ready"), sem("hT_saved")
        q_ready, q_saved = sem("q_ready"), sem("q_saved")
        k_ready, k_saved = sem("k_ready"), sem("k_saved")
        q_high, k_high = sem("q_high"), sem("k_high")
        stacked = [[sem("stacked00"), sem("stacked01")], [sem("stacked10"), sem("stacked11")]]
        v_ready, v_saved = sem("v_ready"), sem("v_saved")
        s_ready = sem("s_ready")
        max_done = sem("max_done")
        exp_done = sem("exp_done")
        pt_ready = sem("pt_ready")
        pt_dve = sem("pt_dve")
        pt_act = sem("pt_act")
        pv_ready = sem("pv_ready")
        rexp_done = sem("rexp_done")
        rbc_ready, rbc_saved = sem("rbc_ready"), sem("rbc_saved")
        onorm_done = sem("onorm_done")
        wo_ready = sem("wo_ready")
        res_done = sem("res_done")
        h2_done = sem("h2_done")
        h2T_ready, h2T_saved = sem("h2T_ready"), sem("h2T_saved")
        log_ready, perm_done = sem("log_ready"), sem("perm_done")
        pbt_ready = sem("pbt_ready")
        pbd_dve, pbd_act = sem("pbd_dve"), sem("pbd_act")
        sel_ready = sem("sel_ready")
        sel_dve, sel_act = sem("sel_dve"), sem("sel_act")
        kept = sem("kept")
        in_ready = sem("in_ready")
        in_dve, in_act = sem("in_dve"), sem("in_act")
        f2_ready = sem("f2_ready")
        st_dve, st_act = sem("st_dve"), sem("st_act")
        moved = [sem("moved0"), sem("moved1")]
        gathered = [sem("gathered0"), sem("gathered1")]
        sc_ready = sem("sc_ready")
        fin_done = sem("fin_done")
        out_done = sem("out_done")

        block = ctx.enter_context(nc.Block())

        def in_loop(n):
            return not isinstance(n, int)

        def batches(eng, body):
            body(0, 0, False)
            body(1, 1, False)
            with eng.Fori(1, B // 2 - 1) as i:
                for par in range(2):
                    body(i * 2 + par, par, False)
            body(B - 2, 0, False)
            body(B - 1, 1, True)

        def xbatch(v, b):
            return v[:, b * QT:b * QT + QT, :] if isinstance(b, int) else v[:, bass.ds(b * QT, QT), :]

        def xtile(i):
            return X1[:, i, :] if isinstance(i, int) else X1[:, bass.ds(i, 1), :].rearrange("p o d -> p (o d)")

        def copy_selected(copy, u, m):
            t, k = divmod(m, 2)
            tile = u * UT + t
            src = bank[4 + (8 * u + m) % 3][:, :].rearrange("p (g e) -> p g e", e=ES)
            return copy(XS[:, k, :, GPT * tile:GPT * tile + GPT].rearrange("p e g -> p g e"), src)

        def one_hot_block(half, j):
            r = slice(32 * j, 32 * j + 32)
            return (permBD[r, half, :, j, :],
                    bank[3][r, half * 2 * P:(half + 1) * 2 * P].rearrange("p (t e) -> p t e", t=2))

        def out_bank(s):
            return bank[(7, 0, 1, 2)[s % 4]]

        def inner_block(q, j):
            r = slice(32 * j, 32 * j + 32)
            return innerBD[r, q % 2, :, j, :], bank[q % 2][r, 0:CG].rearrange("p (g i) -> p g i", g=4)

        @block.sync
        def _(sp):
            for k, W in enumerate((Wq, Wk, Wv, Wo)):
                sp.dma_start(wtmp[:, 2 * k:2 * k + 2, :], W.rearrange("(t p) i -> p t i", p=P)).then_inc(w_in, 16)
            sp.dma_start(adjs, adj.rearrange("(t p) k -> p t k", p=P)).then_inc(w_in, 16)

            def load_x(b, par):
                if in_loop(b) or (b - par) * 8 > 0:
                    sp.wait_ge(x_in[par], (b - par) * 8)
                sp.dma_start(xbatch(X1, b), xbatch(xt, b)).then_inc(x_in[par], 16)

            def stack_parts(b, par):
                sp.wait_ge(q_saved, b + 1)
                sp.wait_ge(k_saved, b + 1)
                for j in range(HPG):
                    src = parts[32 * j:32 * j + 32, :, :, :].rearrange("p s g n -> p s (g n)")
                    for r, chosen in enumerate((slice(0, 3, 2), slice(0, 4, 3), slice(1, 3, 1), slice(1, 4, 2))):
                        sp.dma_start(stack[32 * r:32 * r + 32, par, j, :, :].bitcast(F32), src[:, chosen, :].bitcast(F32))\
                            .then_inc(stacked[par][j // 2], 16)
            for b in range(4):
                load_x(b, b % 2)
            stack_parts(0, 0)
            stack_parts(1, 1)
            with sp.Fori(1, B // 2 - 1) as i:
                for par in range(2):
                    load_x(i * 2 + (2 + par), par)
                for par in range(2):
                    stack_parts(i * 2 + par, par)
            stack_parts(B - 2, 0)
            stack_parts(B - 1, 1)
            sp.dma_start(f1s[:, :, :, :], f1.rearrange("(t p) e s f -> p t (e s) f", p=P)).then_inc(ffn_in, 16)
            for half in range(2):
                sp.dma_start(ctl[:, :, half, :], controller.rearrange("(t p) e s -> p t (e s)", p=P)).then_inc(ffn_in, 16)

            sp.dma_start(f2s[:, :, :], f2.rearrange("e s f d -> (e s f) d").rearrange("(q p) d -> p q d", p=P))\
              .then_inc(ffn_in, 16)
            def move(c, q):
                n = c * QUADS + q
                sp.wait_ge(st_dve, n + 1)
                sp.wait_ge(st_act, n + 1)
                for j in range(4):
                    sp.dma_start(by_group(c, q, j), stage[32 * j:32 * j + 32, q % 2, :, :]).then_inc(moved[q % 2], 16)

            def gather(c, tile):
                if tile < 2:
                    for m in moved:
                        sp.wait_ge(m, (c + 1) * (QUADS // 2) * 64)
                else:
                    if in_loop(c) or c * (CT // 2) + tile // 2 > 0:
                        sp.wait_ge(sc_ready, c * (CT // 2) + tile // 2)
                sp.dma_start(XR[:, tile % 2, :, :], by_expert(c, tile)).then_inc(gathered[tile % 2], 16)

            def store(c, s):
                n = c * (CT // 2) + s
                sp.wait_ge(fin_done, n + 1)
                tiles = slice(2 * n, 2 * n + 2) if isinstance(n, int) else bass.ds(n * 2, 2)
                sp.dma_start(ot[:, tiles, :], X1[:, tiles, :]).then_inc(out_done, 16)

            with sp.Fori(0, CHUNKS - 1) as c:
                for q in range(QUADS):
                    move(c, q)
                for s in range(CT // 2):
                    gather(c, 2 * s)
                    gather(c, 2 * s + 1)
                    if s > 0:
                        store(c, s - 1)
                store(c, CT // 2 - 1)
            for q in range(QUADS):
                move(CHUNKS - 1, q)
            for m in moved:
                sp.wait_ge(m, CHUNKS * (QUADS // 2) * 64)
            for i in range(4):
                rows = slice((CHUNKS - 1) * CG + 4 * GPT * i, (CHUNKS - 1) * CG + 4 * GPT * (i + 1))
                sp.dma_start(XRlast[:, 4 * i:4 * i + 4, :, :].rearrange("p t j d -> p (t j) d"),
                             scratch[rows, :].rearrange("(c two) (e d) -> (two e) c d", two=2, d=D))\
                    .then_inc(last_in[i], 16)
            for s in range(CT // 2):
                store(CHUNKS - 1, s)
            sp.wait_ge(out_done, CHUNKS * (CT // 2) * 16)

        @block.gpsimd
        def _(pool):
            nc.gpsimd.memset(ident[:, :], 0.0).then_inc(consts, 1)
            nc.gpsimd.memset(identb[:, :], 0.0).then_inc(consts, 1)
            pool.wait_ge(consts, 2)
            for m in (ident, identb):
                nc.gpsimd.affine_select(out=m[:, :], in_=m[:, :], compare_op=ALU.not_equal, fill=1.0, base=0,
                                        pattern=[[-1, P]], channel_multiplier=1).then_inc(consts, 1)
            nc.gpsimd.memset(permBD[:, :, :, :, :], 0.0).then_inc(zeroed, 1)
            nc.gpsimd.memset(innerBD[:, :, :, :, :], 0.0).then_inc(zeroed, 1)
            nc.gpsimd.memset(one[:, :, :], 0.0).then_inc(zeroed, 1)
            values = np.linspace(0.0, 1e-6, T).astype(np.float32)
            for t in range(T):
                nc.gpsimd.memset(tie[:, 0, t:t + 1], float(values[t])).then_inc(zeroed, 1)

            pool.wait_ge(bias_done, 1)

            def add_bo(b, par, last):
                pool.wait_ge(ln_done, b + 1)
                xb = xbatch(X1, b)
                nc.gpsimd.tensor_tensor(xb, xb, bob[:, :, :], ALU.add).then_inc(bo_added, 1)
            batches(pool, add_bo)

            def keep(c, u):
                n = c * UNITS + u
                pool.wait_ge(perm_done, n + 1)
                if in_loop(c) or (c - 1) * (CT // 2) + 2 * u + 2 > 0:
                    pool.wait_ge(sc_ready, (c - 1) * (CT // 2) + 2 * u + 2)
                nc.gpsimd.tensor_tensor(permT[:, u * UT * P:(u + 1) * UT * P], one[:, u % 2, :], one[:, u % 2, :],
                                        ALU.mult).then_inc(kept, 1)
            for u in range(UNITS):
                keep(0, u)
            with pool.Fori(1, CHUNKS) as c:
                for u in range(UNITS):
                    keep(c, u)

        @block.tensor
        def _(pe):
            pe.wait_ge(consts, 4)
            pe.wait_ge(w_in, 16 * 9)
            for k in range(4):
                for ob in range(KT):
                    for ib in range(KT):
                        last = nc.tensor.transpose(bank[k][:, ib * D + ob * P:ib * D + ob * P + P],
                                                   wtmp[:, 2 * k + ob, ib * P:ib * P + P], ident[:, :])
                last.then_inc(wt_ready, 1)
            pe.wait_ge(wt_saved, 4)

            pe.wait_ge(setup_dve, 2)
            for k in range(KT):
                last = nc.tensor.matmul(bank[4][:, 0:D], bvx[:, k, :], WT[:, 3, k, :], start=(k == 0), stop=(k == KT - 1))
            last.then_inc(bias_ready, 1)
            pe.wait_ge(bias_done, 1)

            def h_transpose(b):
                pe.wait_ge(ln_done, b + 1)
                if in_loop(b) or b > 0:
                    pe.wait_ge(v_saved, b)
                for t in range(QT):
                    for k in range(KT):
                        last = nc.tensor.transpose(M[0][:, k * N + t * P:k * N + t * P + P],
                                                   hn[:, t, k * P:k * P + P], ident[:, :])
                last.then_inc(hT_ready, 1)

            def project(w, m, ready):
                for g in range(G):
                    for k in range(KT):
                        last = nc.tensor.matmul(m[:, g * N:g * N + N], WT[:, w, k, g * P:g * P + P], hT[:, k, :],
                                                start=(k == 0), stop=(k == KT - 1))
                last.then_inc(ready, 1)

            def q_project(b):
                pe.wait_ge(hT_saved, b + 1)
                if isinstance(b, int) and b < 3:
                    if in_loop(b) or b > 0:
                        pe.wait_ge(q_saved, b)
                else:
                    if in_loop(b) or b - 2 > 0:
                        pe.wait_ge(res_done, b - 2)
                project(0, M[1], q_ready)

            def k_project(b):
                pe.wait_ge(hT_saved, b + 1)
                project(1, M[0], k_ready)

            def v_project(b):
                pe.wait_ge(k_saved, b + 1)
                for t in range(QT):
                    for k in range(KT):
                        last = nc.tensor.matmul(M[0][:, t * D:t * D + D], hT[:, k, t * P:t * P + P], WT[:, 2, k, :],
                                                start=(k == 0), stop=(k == KT - 1))
                last.then_inc(v_ready, 1)

            def scores(b, par, pr):
                if pr < 2:
                    pe.wait_ge(stacked[par][pr], 128 * (b // 2 + 1) if isinstance(b, int) else (b - par) * 64 + 128)
                for t in range(QT):
                    n = 2 * pr + t
                    before = n - 3 if n > 2 else (-2, -1, -3)[n]
                    if in_loop(b) or b * 8 + before + 1 > 0:
                        pe.wait_ge(exp_done, b * 8 + before + 1)
                    s = S[n % 3]
                    nc.tensor.matmul(s[:, :], identb[:, :], maskb[:, t, :, :], start=True, stop=False)
                    for h in range(2):
                        g, j = divmod(2 * pr + h, HPG)
                        last = nc.tensor.matmul(s[:, h * N:h * N + N], stack[:, par, j, 0, g * N + t * P:g * N + t * P + P],
                                                stack[:, par, j, 1, g * N:g * N + N], start=False, stop=(h == 1))
                    last.then_inc(s_ready, 1)

            def p_transpose(b, par, pr):
                pe.wait_ge(exp_done, b * 8 + 2 * pr + 2)
                for h, copied in ((2 * pr, pt_dve), (2 * pr + 1, pt_act)):
                    if in_loop(b) or b * 4 + pr > 0:
                        pe.wait_ge(copied, b * 4 + pr)
                    for k in range(QT):
                        for t in range(QT):
                            last = nc.tensor.transpose(PTb[h % 2][:, k * N + t * P:k * N + t * P + P],
                                                       Ps[:, pr % 2, t, h % 2, k * P:k * P + P], ident[:, :])
                    last.then_inc(pt_ready, 1)

            def pv(b, par, g):
                pe.wait_ge(pt_dve, b * 4 + 2 * g + 2)
                pe.wait_ge(pt_act, b * 4 + 2 * g + 2)
                if g == 0:
                    if in_loop(b) or b > 0:
                        pe.wait_ge(onorm_done, b)
                    pe.wait_ge(v_saved, b + 1)
                for k in range(QT):
                    for j in range(HPG):
                        h = g * HPG + j
                        last = nc.tensor.matmul(Ob[32 * j:32 * j + 32, g * N:g * N + N],
                                                Vs[:, par, k, h * DH:h * DH + DH], PTs[:, h, k * N:k * N + N],
                                                start=(k == 0), stop=(k == QT - 1))
                last.then_inc(pv_ready, 1)

            def r_transpose(b, last):
                pe.wait_ge(rexp_done, b + 1)
                if not last:
                    pe.wait_ge(q_saved, b + 3)
                else:
                    if in_loop(b) or b > 0:
                        pe.wait_ge(res_done, b)
                for g in range(G):
                    for t in range(QT):
                        last = nc.tensor.transpose(M[1][:, g * N + t * P:g * N + t * P + P],
                                                   rexp[:, t, g * P:g * P + P], ident[:, :])
                last.then_inc(rbc_ready, 1)

            def o_project(b):
                pe.wait_ge(onorm_done, b + 1)
                pe.wait_ge(rbc_saved, b + 1)
                for t in range(QT):
                    for g in range(G):
                        last = nc.tensor.matmul(M[1][:, t * D:t * D + D], OT[:, g, t * P:t * P + P], WT[:, 3, g, :],
                                                start=(g == 0), stop=(g == G - 1))
                last.then_inc(wo_ready, 1)

            h_transpose(0)
            q_project(0)
            k_project(0)
            v_project(0)
            h_transpose(1)

            def batch(b, par, last):
                first = isinstance(b, int) and b == 0
                late = isinstance(b, int) and b >= B - 2
                scores(b, par, 0)
                if not last:
                    q_project(b + 1)
                if not first:
                    pv(b - 1, 1 - par, 1)
                if not last:
                    k_project(b + 1)
                scores(b, par, 1)
                if not first:
                    r_transpose(b - 1, last)
                p_transpose(b, par, 0)
                if not last:
                    v_project(b + 1)
                scores(b, par, 2)
                p_transpose(b, par, 1)
                if not first:
                    o_project(b - 1)
                scores(b, par, 3)
                p_transpose(b, par, 2)
                if not late:
                    h_transpose(b + 2)
                pv(b, par, 0)
                p_transpose(b, par, 3)
            batches(pe, batch)
            pv(B - 1, 1, 1)
            r_transpose(B - 1, True)
            o_project(B - 1)

            pe.wait_ge(ffn_in, 16 * 4)
            pe.wait_ge(zeroed, 3 + T)
            pe.wait_ge(res_done, B)

            def unit_transpose(n, par):
                pe.wait_ge(h2_done, n + 1)
                for k in range(KT):
                    for t in range(UT):
                        last = nc.tensor.transpose(bank[k][:, t * P:t * P + P],
                                                   h2[:, par, t, k * P:k * P + P], ident[:, :])
                last.then_inc(h2T_ready, 1)

            def logits(n):
                pe.wait_ge(h2T_saved, n + 1)
                if in_loop(n) or n > 0:
                    pe.wait_ge(perm_done, n)
                for k in range(KT):
                    last = nc.tensor.matmul(bank[2][:, :], ctl[:, k, :, :], h2T[:, k, :],
                                            start=(k == 0), stop=(k == KT - 1))
                last.then_inc(log_ready, 1)

            def one_hot_transpose(n, par):
                pe.wait_ge(perm_done, n + 1)
                if in_loop(n) or 2 * n > 0:
                    pe.wait_ge(pbd_dve, 2 * n)
                if in_loop(n) or 2 * n > 0:
                    pe.wait_ge(pbd_act, 2 * n)
                for t in range(UT):
                    last = nc.tensor.transpose(bank[3][:, t * P:t * P + P],
                                               one[:, par, t * P:t * P + P], ident[:, :])
                last.then_inc(pbt_ready, 1)

            def select(c, u, t):
                n = c * UNITS + u
                half = t // 2
                pe.wait_ge(pbd_dve, 2 * n + half + 1)
                pe.wait_ge(pbd_act, 2 * n + half + 1)
                for k in range(KT):
                    m = 8 * u + 2 * t + k
                    if m >= 3:
                        o = m - 3
                        pe.wait_ge(sel_act if o % 2 else sel_dve, c * 4 * UNITS + o // 2 + 1)
                    elif m == 0:
                        if in_loop(c) or c * QUADS > 0:
                            pe.wait_ge(st_dve, c * QUADS)
                        if in_loop(c) or c * QUADS > 0:
                            pe.wait_ge(st_act, c * QUADS)
                    nc.tensor.matmul(bank[4 + m % 3][:, :], h2[:, u % 2, t, k * P:k * P + P],
                                     permBD[:, half, t % 2, :, :], start=True, stop=True).then_inc(sel_ready, 1)

            def expand(c, q):
                n = c * QUADS + q
                if q > 1:
                    if in_loop(n) or n - 1 > 0:
                        pe.wait_ge(in_dve, n - 1)
                    if in_loop(n) or n - 1 > 0:
                        pe.wait_ge(in_act, n - 1)
                for k in range(KT):
                    for j in range(4):
                        last = nc.tensor.matmul(bank[q % 2][32 * j:32 * j + 32, 0:CG],
                                                f1s[:, k, 4 * q + j, :], XS[:, k, 4 * q + j, :],
                                                start=(k == 0), stop=(k == KT - 1))
                last.then_inc(in_ready, 1)

            def contract(c, q):
                n = c * QUADS + q
                pe.wait_ge(in_dve, n + 1)
                pe.wait_ge(in_act, n + 1)
                for hf in range(2):
                    if q > 1:
                        if in_loop(n) or n - 1 > 0:
                            pe.wait_ge(st_act if hf else st_dve, n - 1)
                    for g in (2 * hf, 2 * hf + 1):
                        last = nc.tensor.matmul(bank[4 + 2 * (q % 2) + hf][:, g % 2 * D:g % 2 * D + D],
                                                innerBD[:, q % 2, g, :, :], f2s[:, q, :], start=True, stop=True)
                    last.then_inc(f2_ready, 1)

            def scatter_last(s):
                if s % 2 == 0:
                    pe.wait_ge(last_in[s // 2], 16)
                if s == 0:
                    pe.wait_ge(kept, CHUNKS * UNITS)
                if s > 3:
                    pe.wait_ge(fin_done, (CHUNKS - 1) * (CT // 2) + s - 3)
                for tt in range(2):
                    for j in range(4):
                        pr = (2 * s + tt) * 4 + j
                        last = nc.tensor.matmul(out_bank(s)[32 * j:32 * j + 32, tt * D:tt * D + D],
                                                permT[:, pr * 32:pr * 32 + 32], XRlast[:, 2 * s + tt, j, :],
                                                start=True, stop=True)
                last.then_inc(sc_ready, 1)

            def scatter(c, s):
                n = c * (CT // 2) + s
                if s == 0:
                    pe.wait_ge(kept, (c + 1) * UNITS)
                if s > 0:
                    pe.wait_ge(fin_done, n)
                for tt in range(2):
                    pe.wait_ge(gathered[tt], (n + 1) * 16)
                    for j in range(4):
                        pr = (2 * s + tt) * 4 + j
                        last = nc.tensor.matmul(bank[7][32 * j:32 * j + 32, tt * D:tt * D + D],
                                                permT[:, pr * 32:pr * 32 + 32], XR[:, tt, j, :],
                                                start=True, stop=True)
                last.then_inc(sc_ready, 1)

            def unit(c, u, front, back):
                n = c * UNITS + u + 1
                select(c, u, 0)
                if front:
                    unit_transpose(n, (u + 1) % 2)
                select(c, u, 1)
                if front:
                    logits(n)
                if back:
                    scatter(c - 1, 2 * u)
                select(c, u, 2)
                if front:
                    one_hot_transpose(n, (u + 1) % 2)
                select(c, u, 3)
                if back:
                    scatter(c - 1, 2 * u + 1)

            def experts(c):
                pe.wait_ge(sel_dve, (c + 1) * UNITS * 4)
                pe.wait_ge(sel_act, (c + 1) * UNITS * 4)
                expand(c, 0)
                for q in range(QUADS):
                    if q + 1 < QUADS:
                        expand(c, q + 1)
                    contract(c, q)

            unit_transpose(0, 0)
            logits(0)
            one_hot_transpose(0, 0)
            for u in range(UNITS):
                unit(0, u, True, False)
            experts(0)
            with pe.Fori(1, CHUNKS - 1) as c:
                for u in range(UNITS):
                    unit(c, u, True, True)
                experts(c)
            for u in range(UNITS):
                unit(CHUNKS - 1, u, u + 1 < UNITS, True)
            experts(CHUNKS - 1)
            for s in range(CT // 2):
                scatter_last(s)

        @block.scalar
        def _(act):
            for t, b in ((bqs, bq), (bks, bk), (bvs, bv)):
                act.dma_start(t[:, :], b.rearrange("(g p) -> p g", p=P), allow_slow_non_contiguous=True).then_inc(w_in, 16)
            act.dma_start(bob[:, :, :], bo.partition_broadcast(P).unsqueeze(1).broadcast_to([P, 2, D])).then_inc(w_in, 16)
            act.wait_ge(w_in, 16 * 9)
            nc.scalar.mul(bqs[:, :], bqs[:, :], SCALE).then_inc(act_chain, 1)
            for k in range(4):
                act.wait_ge(wt_ready, k + 1)
                nc.scalar.mul(WT[:, k, :, :], bank[k][:, :], SCALE if k == 0 else 1.0).then_inc(wt_saved, 1)
            act.wait_ge(act_chain, 1)

            def save_hT(b):
                act.wait_ge(hT_ready, b + 1)
                nc.scalar.copy(hT[:, :, :], M[0][:, :]).then_inc(hT_saved, 1)

            def apply_norm(b):
                act.wait_ge(root_done, b + 1)
                if in_loop(b) or b > 0:
                    act.wait_ge(hT_ready, b)
                for t in range(QT):
                    last = nc.scalar.activation(hn[:, t, :], xtile(b * QT + t), ACT.Identity,
                                                bias=shift[:, t:t + 1], scale=root[:, 1, t:t + 1])
                last.then_inc(ln_done, 1)

            def save_v(b, par):
                act.wait_ge(v_ready, b + 1)
                nc.scalar.copy(Vs[:, par, :, :], M[0][:, :].rearrange("p (t d) -> p t d", t=QT)).then_inc(v_saved, 1)

            def save_high(b, par, which, ready, bias, done):
                act.wait_ge(ready, b + 1)
                if which == 0:
                    for h in range(2):
                        if in_loop(b) or stacked_before(b, par) > 0:
                            act.wait_ge(stacked[1 - par][h], stacked_before(b, par))
                for g in range(G):
                    last = nc.scalar.activation(parts[:, 2 * which, g, :], M[1 - which][:, g * N:g * N + N], ACT.Identity,
                                                bias=bias[:, g:g + 1])
                last.then_inc(done, 1)

            def stacked_before(b, par):
                return 128 * ((b + 1) // 2) if isinstance(b, int) else (b + par) * 64

            def save_q(b, par):
                save_high(b, par, 0, q_ready, bqs, q_high)

            def save_k(b, par):
                save_high(b, par, 1, k_ready, bks, k_high)

            def exps(b, pr):
                if pr < 2:
                    if in_loop(b) or b * 8 + 4 * (pr // 2) + 2 * pr - 2 > 0:
                        act.wait_ge(pt_ready, b * 8 + 4 * (pr // 2) + 2 * pr - 2)
                else:
                    if in_loop(b) or b * 8 + 2 * (pr - 2) + 2 > 0:
                        act.wait_ge(pt_ready, b * 8 + 2 * (pr - 2) + 2)
                if pr == 0:
                    if in_loop(b) or b > 0:
                        act.wait_ge(rexp_done, b)
                for t in range(QT):
                    act.wait_ge(max_done, b * 8 + 2 * pr + t + 1)
                    for h in range(2):
                        last = nc.scalar.activation(Ps[:, pr % 2, t, h, :], S[(2 * pr + t) % 3][:, h * N:h * N + N],
                                                    ACT.Exp, bias=nmax[:, pr % 2, t, h:h + 1],
                                                    accum_out=sums[:, 2 * pr + h, t:t + 1])
                    last.then_inc(exp_done, 1)

            def save_pt(b, h):
                act.wait_ge(pt_ready, b * 8 + h + 1)
                if in_loop(b) or 2 * b + h // 4 - 1 > 0:
                    act.wait_ge(pv_ready, 2 * b + h // 4 - 1)
                nc.scalar.copy(PTs[:, h, :], PTb[h % 2][:, :]).then_inc(pt_act, 1)

            def save_rbc(b):
                act.wait_ge(rbc_ready, b + 1)
                nc.scalar.copy(rbc[:, :, :], M[1][:, :]).then_inc(rbc_saved, 1)

            apply_norm(0)
            save_hT(0)
            save_q(0, 0)
            save_k(0, 0)
            save_v(0, 0)
            apply_norm(1)
            save_hT(1)

            def batch(b, par, last):
                first = isinstance(b, int) and b == 0
                if not first:
                    save_pt(b - 1, 7)
                late = isinstance(b, int) and b >= B - 2
                exps(b, 0)
                if not last:
                    save_q(b + 1, 1 - par)
                    save_k(b + 1, 1 - par)
                exps(b, 1)
                if not first:
                    save_rbc(b - 1)
                save_pt(b, 1)
                if not last:
                    save_v(b + 1, 1 - par)
                exps(b, 2)
                if not late:
                    apply_norm(b + 2)
                save_pt(b, 3)
                exps(b, 3)
                save_pt(b, 5)
                if not late:
                    save_hT(b + 2)
            batches(act, batch)
            save_pt(B - 1, 7)
            save_rbc(B - 1)

            def save_h2T(n):
                act.wait_ge(h2T_ready, n + 1)
                if in_loop(n) or n > 0:
                    act.wait_ge(perm_done, n)
                for k in range(KT):
                    last = nc.scalar.copy(h2T[:, k, :], bank[k][:, :])
                last.then_inc(h2T_saved, 1)

            def save_one_hot(n, half):
                act.wait_ge(pbt_ready, n + 1)
                if in_loop(n) or n * 8 - 4 + 4 * half > 0:
                    act.wait_ge(sel_ready, n * 8 - 4 + 4 * half)
                for j in (0, 1):
                    last = nc.scalar.copy(*one_hot_block(half, j))
                last.then_inc(pbd_act, 1)

            def save_selected(c, u, m):
                act.wait_ge(sel_ready, (c * UNITS + u) * 8 + m + 1)
                copy_selected(nc.scalar.copy, u, m).then_inc(sel_act, 1)

            def unit(c, u, front):
                n = c * UNITS + u + 1
                save_selected(c, u, 1)
                if front:
                    save_h2T(n)
                save_selected(c, u, 3)
                save_selected(c, u, 5)
                if front:
                    save_one_hot(n, 0)
                save_selected(c, u, 7)
                if front:
                    save_one_hot(n, 1)

            def experts(c):
                def save_inner(q):
                    act.wait_ge(in_ready, c * QUADS + q + 1)
                    if in_loop(c) or (c * QUADS + q) * 2 - 2 > 0:
                        act.wait_ge(f2_ready, (c * QUADS + q) * 2 - 2)
                    for j in (0, 1):
                        dst, src = inner_block(q, j)
                        last = nc.scalar.activation(dst, src, ACT.Relu)
                    last.then_inc(in_act, 1)
                save_inner(0)
                for q in range(QUADS):
                    if q + 1 < QUADS:
                        save_inner(q + 1)
                    act.wait_ge(f2_ready, (c * QUADS + q) * 2 + 2)
                    if in_loop(c) or (c * (QUADS // 2) + q // 2) * 64 > 0:
                        act.wait_ge(moved[q % 2], (c * (QUADS // 2) + q // 2) * 64)
                    nc.scalar.copy(stage[:, q % 2, 2:4, :], bank[5 + 2 * (q % 2)][:, :]).then_inc(st_act, 1)

            act.wait_ge(zeroed, 3 + T)
            save_h2T(0)
            save_one_hot(0, 0)
            save_one_hot(0, 1)
            for u in range(UNITS):
                unit(0, u, True)
            experts(0)
            with act.Fori(1, CHUNKS - 1) as c:
                for u in range(UNITS):
                    unit(c, u, True)
                experts(c)
            for u in range(UNITS):
                unit(CHUNKS - 1, u, u + 1 < UNITS)
            experts(CHUNKS - 1)

        @block.vector
        def _(dve):
            chain = [0, 0]

            def link(ins):
                chain[1] += 1
                ins.then_inc(dve_chain, 1)
                dve.wait_ge(dve_chain, chain[0] + chain[1])

            dve.wait_ge(w_in, 16 * 9)
            link(nc.vector.tensor_scalar(adjf, adjs, 0, None, ALU.not_equal))
            link(nc.vector.tensor_reduce(nanv[:, 0, :], adjf, AX.X, ALU.max))
            link(nc.vector.reciprocal(nanv[:, 1, :], nanv[:, 0, :]))
            link(nc.vector.tensor_tensor(nanv[:, 1, :], nanv[:, 1, :], nanv[:, 0, :], ALU.mult))
            for h in range(2):
                last = nc.vector.tensor_scalar(maskb[:, :, h, :], adjf, 0.0, MASKED, ALU.is_equal, ALU.mult)
            last.then_inc(setup_dve, 1)
            nc.vector.tensor_copy(bvx, bvs[:, :].unsqueeze(2).broadcast_to([P, KT, P])).then_inc(setup_dve, 1)
            dve.wait_ge(bias_ready, 1)
            nc.vector.tensor_tensor(bob[:, :, :], bob[:, :, :],
                                    bank[4][:, 0:D].unsqueeze(1).broadcast_to([P, 2, D]), ALU.add).then_inc(bias_done, 1)

            def mark(ins):
                chain[1] += 1
                ins.then_inc(dve_chain, 1)

            def chain_wait():
                dve.wait_ge(dve_chain, chain[0] + chain[1])

            def root_step(i, n, variance):
                X, Y, A, C = (root[:, j, 0:n] for j in range(4))
                if i == 0:
                    return nc.vector.tensor_scalar(X, variance, EPS, None, ALU.add)
                if i == 1:
                    return nc.vector.tensor_scalar(Y.bitcast(I32), X.bitcast(I32), -0.5, float(0x5f3759df),
                                                   ALU.mult, ALU.add)
                if i % 3 == 2:
                    return nc.vector.scalar_tensor_tensor(A, Y, -0.5, Y, ALU.mult, ALU.mult)
                if i % 3 == 0:
                    return nc.vector.tensor_tensor(C, A, X, ALU.mult)
                return nc.vector.scalar_tensor_tensor(Y, C, 1.5, Y, ALU.add, ALU.mult)
            ROOT_STEPS = 11

            def inverse_root(n, variance):
                for i in range(ROOT_STEPS):
                    link(root_step(i, n, variance))

            def sums_of(b, par):
                dve.wait_ge(x_in[par], (b // 2) * 16 + 16 if isinstance(b, int) else (b - par) * 8 + 16)
                nc.vector.memset(newt[:, :], 0.0)
                for t in range(QT):
                    last = nc.vector.bn_stats(stats[:, t, :], xtile(b * QT + t))
                mark(last)

            def mean_variance(dst):
                chain_wait()
                nc.vector.memset(newt[:, :], 0.0)
                for t in range(QT):
                    last = nc.vector.bn_aggr(dst[:, t, :], stats[:, t, :])
                mark(last)

            def step(i, b):
                chain_wait()
                if i == 1:
                    if in_loop(b) or b > 0:
                        dve.wait_ge(ln_done, b)
                if i < ROOT_STEPS:
                    mark(root_step(i, QT, mv[:, :, 1]))
                else:
                    nc.vector.scalar_tensor_tensor(shift[:, :], mv[:, :, 0], -1.0, root[:, 1, 0:QT], ALU.mult, ALU.mult)\
                        .then_inc(root_done, 1)

            def save_low(b, which, g):
                if g == 0:
                    dve.wait_ge((q_high, k_high)[which], b + 1)
                low = nc.vector.scalar_tensor_tensor(parts[:, 2 * which + 1, g, :], M[1 - which][:, g * N:g * N + N],
                                                     (bqs, bks)[which][:, g:g + 1],
                                                     parts[:, 2 * which, g, :].bitcast(F32), ALU.add, ALU.subtract)
                if g == G - 1:
                    low.then_inc((q_saved, k_saved)[which], 1)

            def maximum(b, pr, t):
                n = 2 * pr + t
                dve.wait_ge(s_ready, b * 8 + n + 1)
                if in_loop(b) or b * 8 + n - 3 > 0:
                    dve.wait_ge(exp_done, b * 8 + n - 3)
                nc.vector.tensor_reduce(nmax[:, pr % 2, t, :], S[n % 3][:, :].rearrange("p (h k) -> p h k", h=2),
                                        AX.X, ALU.max, negate=True).then_inc(max_done, 1)

            def save_pt(b, h):
                dve.wait_ge(pt_ready, b * 8 + h + 1)
                if in_loop(b) or 2 * b + h // 4 - 1 > 0:
                    dve.wait_ge(pv_ready, 2 * b + h // 4 - 1)
                nc.vector.tensor_copy(PTs[:, h, :], PTb[h % 2][:, :]).then_inc(pt_dve, 1)

            def reciprocals(b):
                dve.wait_ge(exp_done, b * 8 + 8)
                link(nc.vector.reciprocal(rsum[:, :, :], sums[:, :, :]))
                for t in range(QT):
                    last = nc.vector.tensor_scalar(
                        rexp[:, t, :].rearrange("p (h d) -> p h d", h=HEADS),
                        rsum[:, :, t:t + 1].broadcast_to([P, HEADS, DH]), nanv[:, 1, t:t + 1], None, ALU.mult)
                last.then_inc(rexp_done, 1)

            def normalise(b):
                dve.wait_ge(rbc_saved, b + 1)
                dve.wait_ge(pv_ready, 2 * b + 2)
                nc.vector.tensor_tensor(OT[:, :, :], Ob[:, :].rearrange("p (g q) -> p g q", g=G), rbc[:, :, :],
                                        ALU.mult)\
                    .then_inc(onorm_done, 1)

            def residual(b):
                dve.wait_ge(wo_ready, b + 1)
                dve.wait_ge(bo_added, b + 1)
                xb = xbatch(X1, b)
                nc.vector.tensor_tensor(xb, xb, M[1][:, :].rearrange("p (t d) -> p t d", t=QT), ALU.add)\
                    .then_inc(res_done, 1)

            def sums_of_result(b):
                dve.wait_ge(res_done, b + 1)
                nc.vector.memset(newt[:, :], 0.0)
                for t in range(QT):
                    last = nc.vector.bn_stats(stats[:, t, :], xtile(b * QT + t))
                mark(last)

            def keep_statistics(b):
                chain_wait()
                tiles = slice(b * QT, b * QT + QT) if isinstance(b, int) else bass.ds(b * QT, QT)
                nc.vector.tensor_copy(mv2[:, tiles, :], mvr[:, :, :])

            for b in range(2):
                sums_of(b, b % 2)
                mean_variance(mv)
                for i in range(ROOT_STEPS + 1):
                    step(i, b)
                if b == 0:
                    for which in range(2):
                        for g in range(G):
                            save_low(0, which, g)
            before = chain[1]
            FRONT = 2 + ROOT_STEPS
            BACK = 3
            MARKS = FRONT + BACK

            def batch(b, par, last):
                first = isinstance(b, int) and b == 0
                late = isinstance(b, int) and b >= B - 2

                def norm_step(i):
                    if not late:
                        step(i, b + 2)
                chain[0], chain[1] = (before if first else b * MARKS + (before - BACK + 1)), 0
                if last:
                    chain[0] -= FRONT
                if not first:
                    save_pt(b - 1, 6)
                maximum(b, 0, 0)
                maximum(b, 0, 1)
                if not late:
                    sums_of(b + 2, par)
                if not last:
                    save_low(b + 1, 0, 0)
                if not late:
                    mean_variance(mv)
                if not last:
                    save_low(b + 1, 0, 1)
                norm_step(0)
                if not last:
                    save_low(b + 1, 1, 0)
                norm_step(1)
                if not last:
                    save_low(b + 1, 1, 1)
                norm_step(2)
                maximum(b, 1, 0)
                norm_step(3)
                maximum(b, 1, 1)
                norm_step(4)
                save_pt(b, 0)
                norm_step(5)
                norm_step(6)
                if not first:
                    normalise(b - 1)
                norm_step(7)
                maximum(b, 2, 0)
                norm_step(8)
                norm_step(9)
                maximum(b, 2, 1)
                norm_step(10)
                save_pt(b, 2)
                norm_step(11)
                if not first:
                    residual(b - 1)
                maximum(b, 3, 0)
                if not first:
                    sums_of_result(b - 1)
                maximum(b, 3, 1)
                if not first:
                    mean_variance(mvr)
                save_pt(b, 4)
                if not first:
                    keep_statistics(b - 1)
                reciprocals(b)
            batches(dve, batch)
            chain[0], chain[1] = chain[0] + chain[1], 0
            save_pt(B - 1, 6)
            normalise(B - 1)
            residual(B - 1)
            sums_of_result(B - 1)
            mean_variance(mvr)
            keep_statistics(B - 1)
            mark(nc.vector.memset(rsum[:, :, :], 0.0))
            chain_wait()
            inverse_root(TILES, mv2[:, :, 1])
            base = chain[0] + chain[1]

            def norm_unit(n, par):
                if in_loop(n) or n * 8 - 8 > 0:
                    dve.wait_ge(sel_ready, n * 8 - 8)
                for t in range(UT):
                    tile = n * UT + t
                    if isinstance(n, int):
                        mean, r = mv2[:, tile, 0:1], root[:, 1, tile:tile + 1]
                    else:
                        mean = mv2[:, bass.ds(tile, 1), 0:1].rearrange("p a b -> p (a b)")
                        r = root[:, 1, bass.ds(tile, 1)]
                    last = nc.vector.tensor_scalar(h2[:, par, t, :], xtile(tile), mean, r, ALU.subtract, ALU.mult)
                last.then_inc(h2_done, 1)

            def one_hot(n, par):
                dve.wait_ge(log_ready, n + 1)
                link(nc.vector.tensor_tensor(LT.rearrange("p (g t) -> p g t", t=T),
                                             bank[2][:, :].rearrange("p (g t) -> p g t", t=T),
                                             tie[:, :, :].broadcast_to([P, UT * GPT, T]), ALU.add))
                link(nc.vector.tensor_reduce(gmax[:, :], LT.rearrange("p (g t) -> p g t", t=T), AX.X, ALU.max))
                if in_loop(n) or n - 1 > 0:
                    dve.wait_ge(kept, n - 1)
                for half in range(2):
                    r = slice(64 * half, 64 * half + 64)

                    def own(v):
                        return v.rearrange("p (c two t) -> p c two t", two=2, t=T)[:, :, half, :]
                    top = gmax[r, :].rearrange("p (c two) -> p c two", two=2)[:, :, half:half + 1]
                    last = nc.vector.tensor_tensor(own(one[r, par, :]), own(LT[r, :]),
                                                   top.broadcast_to([64, UT * 4, T]), ALU.is_equal)
                last.then_inc(perm_done, 1)

            def save_one_hot(n, half):
                dve.wait_ge(pbt_ready, n + 1)
                if in_loop(n) or n * 8 - 4 + 4 * half > 0:
                    dve.wait_ge(sel_ready, n * 8 - 4 + 4 * half)
                for j in (2, 3):
                    last = nc.vector.tensor_copy(*one_hot_block(half, j))
                last.then_inc(pbd_dve, 1)

            def save_selected(c, u, m):
                dve.wait_ge(sel_ready, (c * UNITS + u) * 8 + m + 1)
                copy_selected(nc.vector.tensor_copy, u, m).then_inc(sel_dve, 1)

            def in_last(c):
                return isinstance(c, int) and c == CHUNKS - 1

            def finish(c, s):
                n = c * (CT // 2) + s
                dve.wait_ge(sc_ready, n + 1)
                xb = X1[:, 2 * n:2 * n + 2, :] if isinstance(n, int) else X1[:, bass.ds(n * 2, 2), :]
                product = out_bank(s) if in_last(c) else bank[7]
                nc.vector.tensor_tensor(xb, xb, product[:, :].rearrange("p (t d) -> p t d", t=2), ALU.add)\
                    .then_inc(fin_done, 1)

            def unit(c, u, front, back):
                n = c * UNITS + u + 1
                chain[0], chain[1] = (n - 1) * 2 + base + 2, 0
                if front:
                    norm_unit(n, (u + 1) % 2)
                save_selected(c, u, 0)
                save_selected(c, u, 2)
                if front:
                    one_hot(n, (u + 1) % 2)
                save_selected(c, u, 4)
                if back:
                    finish(c - 1, 2 * u)
                if front:
                    save_one_hot(n, 0)
                save_selected(c, u, 6)
                if back:
                    finish(c - 1, 2 * u + 1)
                if front:
                    save_one_hot(n, 1)

            def experts(c):
                def save_inner(q):
                    dve.wait_ge(in_ready, c * QUADS + q + 1)
                    if in_loop(c) or (c * QUADS + q) * 2 - 2 > 0:
                        dve.wait_ge(f2_ready, (c * QUADS + q) * 2 - 2)
                    for j in (2, 3):
                        dst, src = inner_block(q, j)
                        last = nc.vector.tensor_scalar(dst, src, 0.0, None, ALU.max)
                    last.then_inc(in_dve, 1)
                save_inner(0)
                for q in range(QUADS):
                    if q + 1 < QUADS:
                        save_inner(q + 1)
                    dve.wait_ge(f2_ready, (c * QUADS + q) * 2 + 1)
                    if in_loop(c) or (c * (QUADS // 2) + q // 2) * 64 > 0:
                        dve.wait_ge(moved[q % 2], (c * (QUADS // 2) + q // 2) * 64)
                    nc.vector.tensor_copy(stage[:, q % 2, 0:2, :], bank[4 + 2 * (q % 2)][:, :]).then_inc(st_dve, 1)

            dve.wait_ge(zeroed, 3 + T)
            chain[0], chain[1] = base, 0
            norm_unit(0, 0)
            one_hot(0, 0)
            save_one_hot(0, 0)
            save_one_hot(0, 1)
            for u in range(UNITS):
                unit(0, u, True, False)
            experts(0)
            with dve.Fori(1, CHUNKS - 1) as c:
                for u in range(UNITS):
                    unit(c, u, True, True)
                experts(c)
            for u in range(UNITS):
                unit(CHUNKS - 1, u, u + 1 < UNITS, True)
            experts(CHUNKS - 1)
            for s in range(CT // 2):
                finish(CHUNKS - 1, s)

    return nc


_INS = ['x', 'adj', 'L0_gnn_Wq', 'L0_gnn_bq', 'L0_gnn_Wk', 'L0_gnn_bk', 'L0_gnn_Wv', 'L0_gnn_bv', 'L0_gnn_Wo',
        'L0_gnn_bo', 'L0_ffn_controller', 'L0_ffn_f1', 'L0_ffn_f2']


def kernel(**inputs):
    import concourse.bacc as _bacc
    from concourse.bass_utils import run_bass_kernel_spmd as _run

    nc = _bacc.Bacc("TRN2", target_bir_lowering=False, num_devices=1)
    arrays, args = {}, []
    for name in _INS:
        a = np.ascontiguousarray(inputs[name])
        arrays[f"in_{name}"] = a
        args.append(nc.dram_tensor(f"in_{name}", a.shape, mybir.dt.from_np(a.dtype), kind="ExternalInput").ap())
    shape = inputs['x'].shape
    args.append(nc.dram_tensor("out_0", shape, F32, kind="ExternalOutput").ap())
    gnn_moe_kernel(nc, *args)
    r = _run(nc, [arrays], core_ids=[0])
    return r.results[0]["out_0"]
```
